# Optimizing a Trainium2 kernel written in Bass

```python
import numpy as np
import jax
import jax.numpy as jnp

def _softmax(x, axis=-1):
    return jax.nn.softmax(x, axis=axis)

def _gelu(x):
    return jax.nn.gelu(x, approximate=True)

def _silu(x):
    return jax.nn.silu(x)

def _sigmoid(x):
    return jax.nn.sigmoid(x)

def _layernorm(x, axis=-1, eps=1e-05):
    m = jnp.mean(x, axis=axis, keepdims=True)
    v = jnp.var(x, axis=axis, keepdims=True)
    return (x - m) / jnp.sqrt(v + eps)

def _scatter_add(tgt, idx, src, axis=0):
    return tgt.at[idx].add(src)

def _segment_sum(src, seg, n):
    return jax.ops.segment_sum(src, seg, n)
kernel_name = 'mk_flamingo_gated_d1_seqx_r8_4ec20a'

def setup_inputs(seed: int=0):
    np.random.seed(seed)
    _w = jnp.asarray

    def _rec_inputs():
        import jax
        import jax.numpy as jnp
        _rk = jax.random.key(seed)
        x = -0.0002928 + 1 * jax.random.normal(jax.random.fold_in(_rk, 1), (8, 128, 128), jnp.float32)
        _lenS = 128 - jax.random.randint(jax.random.fold_in(_rk, 7), (8,), 0, max(1, 128 // 4) + 1, jnp.int32)
        _lenS2 = 128 - jax.random.randint(jax.random.fold_in(_rk, 8), (8,), 0, max(1, 128 // 4) + 1, jnp.int32)
        _ctx_1024P = jax.random.normal(jax.random.fold_in(_rk, 11), (8, 16, 128), jnp.float32)
        _ctx_1024c = jax.random.dirichlet(jax.random.fold_in(_rk, 511), 0.3 * jnp.ones((16,), jnp.float32), (8, 128))
        _ctx_1024t = jnp.einsum('bsk,bkd->bsd', _ctx_1024c, _ctx_1024P)
        _ctx_1024t = _ctx_1024t * jax.lax.rsqrt(jnp.mean(jnp.square(_ctx_1024t)) + 1e-12) * 0.953939
        ctx_1024 = -1.39393e-06 + 0.999914 * (_ctx_1024t + 0.3 * jax.random.normal(jax.random.fold_in(_rk, 611), (8, 128, 128), jnp.float32))
        _validS = jnp.arange(128)[None, :] < _lenS[:, None]
        _validS2 = jnp.arange(128)[None, :] < _lenS2[:, None]
        _causal = jnp.tril(jnp.ones((128, 128), dtype=bool))
        mask_BxS2_bf0 = jnp.logical_not(jnp.ones((8, 128), dtype=bool))
        _g = jax.random.normal(jax.random.fold_in(_rk, 9001), (2, 1), jnp.float32)
        _g = jnp.sign(_g) * jnp.maximum(jnp.abs(_g), 1.0) + (_g == 0) * 1.0
        g_xattn = _g[0]
        g_ffn = _g[1]
        return (x, ctx_1024, mask_BxS2_bf0, g_xattn, g_ffn)
    x, ctx_1024, mask_BxS2_bf0, g_xattn, g_ffn = _rec_inputs()

    def _L0_xattn_setup():
        import jax, jax.numpy as jnp
        import numpy as np
        DIM = 128
        HEADS = 16
        DIM_HEAD = 64
        INNER = HEADS * DIM_HEAD
        B, N = (2, 256)
        SCALE = DIM_HEAD ** (-0.5)
        key = jax.random.key(seed)
        ks = jax.random.split(key, 9)
        s_in = 1.0 / np.sqrt(DIM)
        s_inner = 1.0 / np.sqrt(INNER)
        return {'q': jax.random.normal(ks[0], (B, N, DIM), jnp.float32), 'k': jax.random.normal(ks[1], (B, N, DIM), jnp.float32), 'v': jax.random.normal(ks[2], (B, N, DIM), jnp.float32), 'Wq': jax.random.normal(ks[3], (DIM, INNER), jnp.float32) * s_in, 'Wk': jax.random.normal(ks[4], (DIM, INNER), jnp.float32) * s_in, 'Wv': jax.random.normal(ks[5], (DIM, INNER), jnp.float32) * s_in, 'Wo': jax.random.normal(ks[6], (INNER, DIM), jnp.float32) * s_inner, 'bo': jax.random.normal(ks[7], (DIM,), jnp.float32) * s_inner, 'mask': jnp.zeros((B, N), dtype=bool)}
    _L0_xattn_all = _L0_xattn_setup()
    _L0_xattn_in = {k: v for k, v in _L0_xattn_all.items() if k in ('Wq', 'Wk', 'Wv', 'Wo', 'bo')}
    del _L0_xattn_all

    def _L0_ffn_setup():
        import jax, jax.numpy as jnp
        import numpy as np
        import math
        B, T, D, H, E, TOPK, CAPF = (4, 256, 128, 16, 8, 2, 2.0)
        HD = D // H

        def layernorm(x, g, b, eps=1e-05):
            m = jnp.mean(x, -1, keepdims=True)
            v = jnp.mean(jnp.square(x - m), -1, keepdims=True)
            return (x - m) * jax.lax.rsqrt(v + eps) * g + b

        def block_forward(x, ln1_g, ln1_b, Wqkv, Wproj, ln2_g, ln2_b, Wgate, W1, b1, W2, b2):
            Bb, Tt, d = x.shape
            hd = HD
            half = hd // 2
            h = layernorm(x, ln1_g, ln1_b)
            qkv = (h @ Wqkv).reshape(Bb, Tt, H, 3 * hd)
            q, k, v = (qkv[..., :hd], qkv[..., hd:2 * hd], qkv[..., 2 * hd:])
            inv_freq = 1.0 / 10000.0 ** (jnp.arange(0, hd, 2, dtype=jnp.float32) / hd)
            ang = jnp.arange(Tt, dtype=jnp.float32)[:, None] * inv_freq
            sin = jnp.sin(ang)[None, :, None, :].astype(x.dtype)
            cos = jnp.cos(ang)[None, :, None, :].astype(x.dtype)

            def rope(t):
                t1, t2 = (t[..., :half], t[..., half:])
                return jnp.concatenate([t1 * cos - t2 * sin, t1 * sin + t2 * cos], -1)
            q, k = (rope(q), rope(k))
            scores = jnp.einsum('bqhd,bkhd->bhqk', q, k) / math.sqrt(hd)
            causal = jnp.tril(jnp.ones((Tt, Tt), dtype=bool))
            scores = jnp.where(causal, scores, jnp.asarray(-1000000000.0, scores.dtype))
            probs = jax.nn.softmax(scores, axis=-1)
            attn = jnp.einsum('bhqk,bkhd->bqhd', probs, v).reshape(Bb, Tt, d) @ Wproj
            x = x + attn
            h2 = layernorm(x, ln2_g, ln2_b)
            flat = h2.reshape(-1, d)
            N = flat.shape[0]
            capacity = int(math.ceil(CAPF * N / E))
            gates = jax.nn.softmax((flat @ Wgate).astype(jnp.float32), -1).astype(flat.dtype)
            _, top_inds = jax.lax.top_k(gates, TOPK)
            mask = jnp.zeros((N, E), dtype=bool).at[jnp.arange(N)[:, None], top_inds].set(True)
            pos = jnp.cumsum(mask.astype(jnp.int32), axis=0) * mask - 1
            keep = (pos < capacity) & mask
            t_flat = jnp.repeat(jnp.arange(N), TOPK)
            e_flat = top_inds.reshape(-1)
            p = pos[t_flat, e_flat]
            kp = keep[t_flat, e_flat]
            p_eff = jnp.where(kp, p, capacity)
            exp_in = jnp.zeros((E, capacity, d), flat.dtype).at[e_flat, p_eff].set(flat[t_flat], mode='drop')
            hmid = jax.nn.gelu(jnp.einsum('ecd,edf->ecf', exp_in, W1) + b1[:, None, :], approximate=False)
            exp_out = jnp.einsum('ecf,efd->ecd', hmid, W2) + b2[:, None, :]
            gate = gates[t_flat, e_flat] * kp.astype(flat.dtype)
            p_g = jnp.minimum(p_eff, capacity - 1)
            moe = jnp.zeros((N, d), flat.dtype).at[t_flat].add(exp_out[e_flat, p_g] * gate[:, None])
            return x + moe.reshape(Bb, Tt, d)
        key = jax.random.key(seed)
        ks = jax.random.split(key, 8)
        s = 0.02
        return {'x': jax.random.normal(ks[0], (B, T, D), jnp.float32), 'ln1_g': jnp.ones((D,), jnp.float32), 'ln1_b': jnp.zeros((D,), jnp.float32), 'Wqkv': jax.random.normal(ks[1], (D, 3 * D), jnp.float32) * s, 'Wproj': jax.random.normal(ks[2], (D, D), jnp.float32) * s, 'ln2_g': jnp.ones((D,), jnp.float32), 'ln2_b': jnp.zeros((D,), jnp.float32), 'Wgate': jax.random.normal(ks[3], (D, E), jnp.float32) * s, 'W1': jax.random.normal(ks[4], (E, D, 4 * D), jnp.float32) * s, 'b1': jnp.zeros((E, 4 * D), jnp.float32), 'W2': jax.random.normal(ks[5], (E, 4 * D, D), jnp.float32) * s, 'b2': jnp.zeros((E, D), jnp.float32)}
    _L0_ffn_all = _L0_ffn_setup()
    _L0_ffn_in = {k: v for k, v in _L0_ffn_all.items() if k in ('ln1_g', 'ln1_b', 'Wqkv', 'Wproj', 'ln2_g', 'ln2_b', 'Wgate', 'W1', 'b1', 'W2', 'b2')}
    del _L0_ffn_all
    return {'x': x, 'ctx_1024': ctx_1024, 'mask_BxS2_bf0': mask_BxS2_bf0, 'g_xattn': g_xattn, 'g_ffn': g_ffn, 'L0_xattn_Wq': _L0_xattn_in['Wq'], 'L0_xattn_Wk': _L0_xattn_in['Wk'], 'L0_xattn_Wv': _L0_xattn_in['Wv'], 'L0_xattn_Wo': _L0_xattn_in['Wo'], 'L0_xattn_bo': _L0_xattn_in['bo'], 'L0_ffn_ln1_g': _L0_ffn_in['ln1_g'], 'L0_ffn_ln1_b': _L0_ffn_in['ln1_b'], 'L0_ffn_Wqkv': _L0_ffn_in['Wqkv'], 'L0_ffn_Wproj': _L0_ffn_in['Wproj'], 'L0_ffn_ln2_g': _L0_ffn_in['ln2_g'], 'L0_ffn_ln2_b': _L0_ffn_in['ln2_b'], 'L0_ffn_Wgate': _L0_ffn_in['Wgate'], 'L0_ffn_W1': _L0_ffn_in['W1'], 'L0_ffn_b1': _L0_ffn_in['b1'], 'L0_ffn_W2': _L0_ffn_in['W2'], 'L0_ffn_b2': _L0_ffn_in['b2']}

def reference(x, ctx_1024, mask_BxS2_bf0, g_xattn, g_ffn, L0_xattn_Wq, L0_xattn_Wk, L0_xattn_Wv, L0_xattn_Wo, L0_xattn_bo, L0_ffn_ln1_g, L0_ffn_ln1_b, L0_ffn_Wqkv, L0_ffn_Wproj, L0_ffn_ln2_g, L0_ffn_ln2_b, L0_ffn_Wgate, L0_ffn_W1, L0_ffn_b1, L0_ffn_W2, L0_ffn_b2):
    import jax
    import jax.numpy as jnp

    def _L0_xattn_ref(q, k, v, Wq, Wk, Wv, Wo, bo, mask):
        import jax, jax.numpy as jnp
        import numpy as np
        DIM = 128
        HEADS = 16
        DIM_HEAD = 64
        INNER = HEADS * DIM_HEAD
        B, N = (2, 256)
        SCALE = DIM_HEAD ** (-0.5)
        b, n, _ = q.shape
        h, d = (HEADS, DIM_HEAD)

        def split_heads(x):
            return x.reshape(b, n, h, d).transpose(0, 2, 1, 3)
        qh = split_heads(q @ Wq)
        kh = split_heads(k @ Wk)
        vh = split_heads(v @ Wv)
        dots = jnp.einsum('bhid,bhjd->bhij', qh, kh) * SCALE
        mask_value = -jnp.finfo(dots.dtype).max
        dots = jnp.where(mask[:, None, None, :], mask_value, dots)
        causal = jnp.triu(jnp.ones((n, n), dtype=bool), k=1)
        dots = jnp.where(causal[None, None, :, :], mask_value, dots)
        attn = jax.nn.softmax(dots, axis=-1)
        out = jnp.einsum('bhij,bhjd->bhid', attn, vh)
        out = out.transpose(0, 2, 1, 3).reshape(b, n, h * d)
        return out @ Wo + bo

    def _L0_ffn_ref(x, ln1_g, ln1_b, Wqkv, Wproj, ln2_g, ln2_b, Wgate, W1, b1, W2, b2):
        import jax, jax.numpy as jnp
        import numpy as np
        import math
        B, T, D, H, E, TOPK, CAPF = (4, 256, 128, 16, 8, 2, 2.0)
        HD = D // H

        def layernorm(x, g, b, eps=1e-05):
            m = jnp.mean(x, -1, keepdims=True)
            v = jnp.mean(jnp.square(x - m), -1, keepdims=True)
            return (x - m) * jax.lax.rsqrt(v + eps) * g + b

        def block_forward(x, ln1_g, ln1_b, Wqkv, Wproj, ln2_g, ln2_b, Wgate, W1, b1, W2, b2):
            Bb, Tt, d = x.shape
            hd = HD
            half = hd // 2
            h = layernorm(x, ln1_g, ln1_b)
            qkv = (h @ Wqkv).reshape(Bb, Tt, H, 3 * hd)
            q, k, v = (qkv[..., :hd], qkv[..., hd:2 * hd], qkv[..., 2 * hd:])
            inv_freq = 1.0 / 10000.0 ** (jnp.arange(0, hd, 2, dtype=jnp.float32) / hd)
            ang = jnp.arange(Tt, dtype=jnp.float32)[:, None] * inv_freq
            sin = jnp.sin(ang)[None, :, None, :].astype(x.dtype)
            cos = jnp.cos(ang)[None, :, None, :].astype(x.dtype)

            def rope(t):
                t1, t2 = (t[..., :half], t[..., half:])
                return jnp.concatenate([t1 * cos - t2 * sin, t1 * sin + t2 * cos], -1)
            q, k = (rope(q), rope(k))
            scores = jnp.einsum('bqhd,bkhd->bhqk', q, k) / math.sqrt(hd)
            causal = jnp.tril(jnp.ones((Tt, Tt), dtype=bool))
            scores = jnp.where(causal, scores, jnp.asarray(-1000000000.0, scores.dtype))
            probs = jax.nn.softmax(scores, axis=-1)
            attn = jnp.einsum('bhqk,bkhd->bqhd', probs, v).reshape(Bb, Tt, d) @ Wproj
            x = x + attn
            h2 = layernorm(x, ln2_g, ln2_b)
            flat = h2.reshape(-1, d)
            N = flat.shape[0]
            capacity = int(math.ceil(CAPF * N / E))
            gates = jax.nn.softmax((flat @ Wgate).astype(jnp.float32), -1).astype(flat.dtype)
            _, top_inds = jax.lax.top_k(gates, TOPK)
            mask = jnp.zeros((N, E), dtype=bool).at[jnp.arange(N)[:, None], top_inds].set(True)
            pos = jnp.cumsum(mask.astype(jnp.int32), axis=0) * mask - 1
            keep = (pos < capacity) & mask
            t_flat = jnp.repeat(jnp.arange(N), TOPK)
            e_flat = top_inds.reshape(-1)
            p = pos[t_flat, e_flat]
            kp = keep[t_flat, e_flat]
            p_eff = jnp.where(kp, p, capacity)
            exp_in = jnp.zeros((E, capacity, d), flat.dtype).at[e_flat, p_eff].set(flat[t_flat], mode='drop')
            hmid = jax.nn.gelu(jnp.einsum('ecd,edf->ecf', exp_in, W1) + b1[:, None, :], approximate=False)
            exp_out = jnp.einsum('ecf,efd->ecd', hmid, W2) + b2[:, None, :]
            gate = gates[t_flat, e_flat] * kp.astype(flat.dtype)
            p_g = jnp.minimum(p_eff, capacity - 1)
            moe = jnp.zeros((N, d), flat.dtype).at[t_flat].add(exp_out[e_flat, p_g] * gate[:, None])
            return x + moe.reshape(Bb, Tt, d)
        return block_forward(x, ln1_g, ln1_b, Wqkv, Wproj, ln2_g, ln2_b, Wgate, W1, b1, W2, b2)
    x = x + jnp.tanh(g_xattn[0]) * _L0_xattn_ref(_layernorm(x, axis=-1), ctx_1024, ctx_1024, L0_xattn_Wq, L0_xattn_Wk, L0_xattn_Wv, L0_xattn_Wo, L0_xattn_bo, mask_BxS2_bf0)
    x = x + jnp.tanh(g_ffn[0]) * _L0_ffn_ref(_layernorm(x, axis=-1), L0_ffn_ln1_g, L0_ffn_ln1_b, L0_ffn_Wqkv, L0_ffn_Wproj, L0_ffn_ln2_g, L0_ffn_ln2_b, L0_ffn_Wgate, L0_ffn_W1, L0_ffn_b1, L0_ffn_W2, L0_ffn_b2)
    return x

_drawn_inputs = setup_inputs


def setup_inputs(seed=0):
    import zlib

    import numpy as np

    out = dict(_drawn_inputs(seed))
    spreads = {'L0_ffn_ln1_g': (1.0, 0.6),
     'L0_ffn_ln1_b': (0.0, 0.1),
     'L0_ffn_ln2_g': (1.0, 0.2),
     'L0_ffn_ln2_b': (0.0, 0.1),
     'L0_ffn_b1': (0.0, 0.309),
     'L0_ffn_b2': (0.0, 0.1)}
    factors = {}
    for name, (base, spread) in spreads.items():
        noise = np.random.default_rng([zlib.crc32(name.encode()), seed]).standard_normal(out[name].shape)
        drawn = base * np.exp(spread * noise) if base else spread * noise
        out[name] = jnp.asarray(drawn.astype(out[name].dtype))
    for name, factor in factors.items():
        out[name] = (out[name] * factor).astype(out[name].dtype)
    return out
```

```python
from contextlib import ExitStack

import concourse.bass as bass
from concourse import mybir

F32 = mybir.dt.float32
BF16 = mybir.dt.bfloat16
U32 = mybir.dt.uint32
I32 = mybir.dt.int32
ALU = mybir.AluOpType
ACT = mybir.ActivationFunctionType
AX = mybir.AxisListType

P = 128
NB = 8
XH, XD = 16, 64
INNER = XH * XD
SH, SD = 16, 8
NE, FF = 8, 512
TOPK = 2
CAP = 2 * NB * P // NE
CHUNKS, HC = 4, 4
EPS = 1e-5
NEG = -(2.0 - 2.0 ** -7) * 2.0 ** 127
LAG = 2
RING = 4
MT = FF // P

C_ID, C_CAUSAL, C_TRI = 0, P, 2 * P
C_COS = 3 * P
C_SIN = C_COS + 2 * P
C_HMASK = C_SIN + 2 * P
C_IOTA = C_HMASK + HC
C_TRASH = C_IOTA + 2 * NE
C_POW = C_TRASH + 2 * NB
NCONST = C_POW + NB

LOOP = True


class Signal:

    def __init__(self, sem, per):
        self.sem, self.per = sem, per

    def wait(self, eng, batch, k=None, carrier=None):
        eng.wait_ge(self.sem, batch * self.per + (self.per if k is None else k))
        if carrier is not None and not isinstance(batch, int):
            carrier()


class Chain:

    def __init__(self, eng, rises):
        self.eng, self.rises, self.n = eng, rises, 0

    def start(self, batch):
        self.batch, self.n = batch, 0

    def link(self, ins, carrier=None):
        self.n += 1
        ins.then_inc(self.rises.sem, 1)
        self.rises.wait(self.eng, self.batch, self.n, carrier)

    def end(self):
        assert self.n == self.rises.per, (self.n, self.rises.per)


def build(nc, x, ctx_in, mask, g_x, g_f, wq, wk, wv, wo, bo, ln1_g, ln1_b, wqkv, wproj, ln2_g, ln2_b,
          wgate, w1, b1, w2, b2, const, out):
    stack = ExitStack()
    with stack:
        def sb(name, shape, dt=F32):
            return stack.enter_context(nc.sbuf_tensor(name, shape, dt))

        def bank(name):
            return stack.enter_context(nc.psum_tensor(name, [P, 512], F32))

        def sem(name):
            return stack.enter_context(nc.semaphore(name))

        def signal(name, per):
            return Signal(sem(name), per)

        queue_in = nc.dram_tensor("queue_in", [NE * CAP + NB * P * TOPK, P], F32).ap()
        queue_out = nc.dram_tensor("queue_out", [NE * CAP, P], F32).ap()

        cst = sb("cst", [P, NCONST])
        ident = cst[:, C_ID:C_ID + P]
        cos_qk, sin_qk = cst[:, C_COS:C_COS + 2 * P], cst[:, C_SIN:C_SIN + 2 * P]
        iota2 = cst[:, C_IOTA:C_IOTA + 2 * NE].rearrange("p (k e) -> p k e", k=2)
        ident_bf = sb("ident_bf", [P, P], BF16)
        causal_bf = sb("causal_bf", [P, P], BF16)
        tri_bf = sb("tri_bf", [P, P], BF16)
        ones_bf = sb("ones_bf", [P, P], BF16)
        mask_i32 = sb("mask_i32", [P, NB * P], I32)
        mask_neg = sb("mask_neg", [P, NB * P], BF16)
        mask_all = sb("mask_all", [P, NB * P], BF16)
        x_all = sb("x_all", [P, NB, P])
        x1_all = sb("x1_all", [P, NB, P])
        z_all = sb("z_all", [P, NB, P])
        wq_sb, wk_sb, wv_sb = sb("wq_sb", [P, INNER]), sb("wk_sb", [P, INNER]), sb("wv_sb", [P, INNER])
        wo_sb = sb("wo_sb", [P, INNER // P, P])
        bo_bc = sb("bo_bc", [P, P])
        wqkv_sb = sb("wqkv_sb", [P, 3 * P])
        w4_sb = sb("w4_sb", [P, 4, P])
        wvs_sb = sb("wvs_sb", [P, P])
        wproj_sb = sb("wproj_sb", [P, P])
        wgate_sb = sb("wgate_sb", [P, NE])
        gates2 = sb("gates2", [P, 2])
        tanh2 = sb("tanh2", [P, 2])
        NV = 4 + NE * MT
        rows = sb("rows", [NV, P])
        cols = sb("cols", [P, NV])
        zero = sb("zero", [P, 512])
        stats_x = sb("stats_x", [P, NB, 6])
        mv_x = sb("mv_x", [P, NB, 2])
        ve_x = sb("ve_x", [P, NB])
        rstd_x = sb("rstd_x", [P, NB])

        tiny = sb("tiny", [P, 3])

        xn = sb("xn", [P, P])
        c_sb = sb("c_sb", [P, P])
        xcT = sb("xcT", [P, 2 * P])
        qT, kT = sb("qT", [P, INNER // P, P]), sb("kT", [P, INNER // P, P])
        v_sb = sb("v_sb", [P, INNER])
        nmax_a, nmax_b = sb("nmax_a", [P, XH]), sb("nmax_b", [P, SH])
        sum_a, sum_b = sb("sum_a", [P, XH]), sb("sum_b", [P, SH])
        rec_a, rec_b = sb("rec_a", [P, XH]), sb("rec_b", [P, SH])
        p_a, p_b = sb("p_a", [P, 2, HC, P]), sb("p_b", [P, 2, HC, P])
        pT_a, pT_b = sb("pT_a", [P, HC, P]), sb("pT_b", [P, HC, P])
        oT_a = sb("oT_a", [P, 4, P])
        st_a, mv_a, ve_a, rs_a = sb("st_a", [P, 2, 6]), sb("mv_a", [P, 2, 2]), sb("ve_a", [P, 2]), sb("rs_a", [P, 2])

        h_sb = sb("h_sb", [P, P])
        hT = sb("hT", [P, P])
        rope1, rope2 = sb("rope1", [P, 2 * P]), sb("rope2", [P, 2 * P])
        qk = sb("qk", [P, 2, P])
        km = sb("km", [P, HC, P])
        v_pad = sb("v_pad", [P, SH, HC * SD])
        oT_b = sb("oT_b", [P, P])
        st_b, mv_b, ve_b, rs_b = sb("st_b", [P, 6]), sb("mv_b", [P, 2]), sb("ve_b", [P, 1]), sb("rs_b", [P, 1])

        h2n = sb("h2n", [P, P])
        h2s = sb("h2s", [P, P])
        h2T = sb("h2T", [P, P])
        r_nmax, r_exp, r_sum, r_rec = sb("r_nmax", [P, 1]), sb("r_exp", [P, NE]), sb("r_sum", [P, 1]), sb("r_rec", [P, 1])
        r_gate, r_top, r_idx, r_idxf = sb("r_gate", [P, NE]), sb("r_top", [P, 8]), sb("r_idx", [P, 8], U32), sb("r_idxf", [P, TOPK])
        r_mk = sb("r_mk", [P, TOPK, NE])
        r_mask = sb("r_mask", [P, NE], BF16)
        r_acc = sb("r_acc", [P, NE], BF16)
        r_pm = sb("r_pm", [P, TOPK, NE])
        r_pos = sb("r_pos", [P, TOPK])
        r_keep, r_kept, r_drop, r_row, r_pmin = (sb(n, [P, TOPK]) for n in ("r_keep", "r_kept", "r_drop", "r_row", "r_pmin"))
        r_slot = sb("r_slot", [P, TOPK], U32)
        gate_all = sb("gate_all", [P, NB, TOPK])
        from_all = sb("from_all", [P, NB, TOPK], U32)

        w1_sb = sb("w1_sb", [P, RING, FF])
        w2_sb = sb("w2_sb", [P, RING, MT, P])
        b2_bc = sb("b2_bc", [P, NE, P])
        xin = sb("xin", [P, RING, 2, P])
        xT = sb("xT", [P, 2, 2 * P])
        hid = sb("hid", [P, 2, MT, 2 * P])
        eo = sb("eo", [P, 2, 2, P])
        got = sb("got", [P, NB, TOPK, P])
        acc = sb("acc", [P, 2, P])
        res = sb("res", [P, NB, P])

        bk = [bank(f"bank{n}") for n in range(8)]
        s_a, s_b, t_a, t_b, o_a, b_misc, y_bank, c_bank = bk
        q_banks, k_banks, v_banks = (s_a, s_b), (t_a, t_b), (c_bank, y_bank)

        d_x, d_cst, d_rows, d_small, d_mask = sem("d_x"), sem("d_cst"), sem("d_rows"), sem("d_small"), sem("d_mask")
        d_wq, d_wk, d_wv, d_wo, d_wqkv = sem("d_wq"), sem("d_wk"), sem("d_wv"), sem("d_wo"), sem("d_wqkv")
        d_zero, d_b2 = sem("d_zero"), sem("d_b2")
        d_ctx = signal("d_ctx", 16)
        zeroed, prep_pool = sem("zeroed"), sem("prep_pool")
        prep = sem("prep")
        consts_ready, vars_ready, rstd_ready = sem("consts_ready"), sem("vars_ready"), sem("rstd_ready")
        rows_turned, cols_ready, tanh_ready = sem("rows_turned"), sem("cols_ready"), sem("tanh_ready")
        xb_ready, w4_ready = sem("xb_ready"), sem("w4_ready")
        xn_ready = signal("xn_ready", 1)
        xc_turned = signal("xc_turned", 1)
        xcT_ready = signal("xcT_ready", 1)
        q_made, k_made, v_made = signal("q_made", 2), signal("k_made", 2), signal("v_made", 2)
        q_ready, k_ready = signal("q_ready", 2), signal("k_ready", 2)
        v_ready0, v_ready1 = signal("v_ready0", 1), signal("v_ready1", 1)
        a_scores, a_max, a_exp, a_rec, a_norm = (signal(n, CHUNKS) for n in ("a_scores", "a_max", "a_exp", "a_rec", "a_norm"))
        a_turned, a_pT, a_pv = (signal(n, CHUNKS) for n in ("a_turned", "a_pT", "a_pv"))
        a_oT = signal("a_oT", 2)
        a_y = signal("a_y", 1)
        a_x1 = signal("a_x1", 1)
        a_chain = signal("a_chain", 5)
        a_var = signal("a_var", 2)
        a_rstd = signal("a_rstd", 2)
        h_ready = signal("h_ready", 1)
        h_turned, hT_ready = signal("h_turned", 1), signal("hT_ready", 1)
        qk_made, qk_read, qkm_ready = signal("qk_made", 1), signal("qk_read", 1), signal("qkm_ready", 1)
        vs_made, vs_ready = signal("vs_made", 1), signal("vs_ready", 1)
        b_scores, b_max, b_exp, b_rec, b_norm = (signal(n, CHUNKS) for n in ("b_scores", "b_max", "b_exp", "b_rec", "b_norm"))
        b_turned, b_pT = signal("b_turned", CHUNKS), signal("b_pT", CHUNKS)
        b_pv, b_oT, b_proj = signal("b_pv", 1), signal("b_oT", 1), signal("b_proj", 1)
        b_chain, b_var, b_rstd, h2n_ready = signal("b_chain", 4), signal("b_var", 1), signal("b_rstd", 1), signal("h2n_ready", 1)
        h2_turned, h2T_ready = signal("h2_turned", 1), signal("h2T_ready", 1)
        logits_made, lmax_ready, lexp_ready = signal("logits_made", 1), signal("lmax_ready", 1), signal("lexp_ready", 1)
        choice_ready, pos_made, pos_read = signal("choice_ready", 1), signal("pos_made", 1), signal("pos_read", 1)
        c_chain, slots_ready = signal("c_chain", 12), signal("slots_ready", 1)
        h2s_ready = signal("h2s_ready", 1)
        d_scatter = signal("d_scatter", 32)
        d_w = [signal(f"d_w{n}", 32) for n in range(RING)]
        d_xin = [signal(f"d_xin{n}", 16) for n in range(RING)]
        d_eo = [signal(f"d_eo{n}", 16) for n in range(2)]
        x_turned, xT_ready, h_made, h_act = signal("x_turned", 1), signal("xT_ready", 1), signal("h_made", 2), signal("h_act", MT)
        e_made, eo_ready = signal("e_made", 1), signal("eo_ready", 1)
        d_got, d_out = [signal(f"d_got{n}", 32) for n in range(NB)], sem("d_out")
        mix_chain, mixed = signal("mix_chain", 2), signal("mixed", 1)

        def batches(eng, body):
            def step(i):
                fixed = isinstance(i, int)
                body(i if not fixed or i < NB else None,
                     i - 1 if not fixed or 0 <= i - 1 < NB else None,
                     i - 2 if not fixed or 0 <= i - 2 < NB else None)
            if LOOP:
                for i in range(3):
                    step(i)
                with eng.Fori(3, NB - 1) as i:
                    step(i)
                for i in range(NB - 1, NB + 2):
                    step(i)
            else:
                for i in range(NB + 2):
                    step(i)

        def has_next(a):
            return not isinstance(a, int) or a + 1 < NB

        def later(batch):
            return not isinstance(batch, int) or batch > 0

        def experts(eng, body):
            if LOOP:
                body(0, 0)
                for j in range(1, RING):
                    body(j, j)
                for j in range(RING):
                    body(RING + j, j)
            else:
                for e in range(NE):
                    body(e, e % RING)

        block = stack.enter_context(nc.Block())

        @block.sync
        def _(sp):
            sp.dma_start(x_all[:], x.rearrange("b t d -> t b d")).then_inc(d_x, 16)
            sp.dma_start(c_sb[:], ctx_in[0]).then_inc(d_ctx.sem, 16)
            sp.dma_start(wq_sb[:], wq).then_inc(d_wq, 16)
            sp.dma_start(wk_sb[:], wk).then_inc(d_wk, 16)
            sp.dma_start(wv_sb[:], wv).then_inc(d_wv, 16)
            sp.dma_start(wqkv_sb[:], wqkv).then_inc(d_wqkv, 16)
            sp.dma_start(wo_sb[:], wo.rearrange("(t p) d -> p t d", p=P)).then_inc(d_wo, 16)
            sp.wait_ge(zeroed, 1)
            for n in range(NE * CAP * P // (P * 512)):
                sp.dma_start(queue_in[n * 512:(n + 1) * 512, :].rearrange("(p r) d -> p (r d)", p=P),
                             zero[:]).then_inc(d_zero, 16)
            sp.dma_start(b2_bc[:].rearrange("p e d -> p (e d)"),
                         b2.rearrange("(o e) d -> o (e d)", o=1).partition_broadcast(P)).then_inc(d_b2, 16)

            def weights(e, j):
                sp.dma_start(w1_sb[:, j, :], w1[e]).then_inc(d_w[j].sem, 16)
                sp.dma_start(w2_sb[:, j, :, :], w2[e].rearrange("(m p) d -> p m d", p=P)).then_inc(d_w[j].sem, 16)

            def body(a, b, c):
                if a is not None and has_next(a):
                    xc_turned.wait(sp, a)
                    sp.dma_start(c_sb[:], ctx_in[a + 1]).then_inc(d_ctx.sem, 16)
            batches(sp, body)
            for e in range(RING):
                weights(e, e)
            d_scatter.wait(sp, NB - 1)
            for e in range(NE):
                if e >= RING:
                    e_made.wait(sp, e - RING)
                    weights(e, e % RING)
                sp.dma_start(xin[:, e % RING, :, :],
                             queue_in[e * CAP:(e + 1) * CAP, :].rearrange("(t p) d -> p t d", p=P)).then_inc(d_xin[e % RING].sem, 16)
            for n in range(NB):
                mixed.wait(sp, n)
                sp.dma_start(out[n], res[:, n, :]).then_inc(d_out, 16)
            sp.wait_ge(d_out, 16 * NB)

        @block.gpsimd
        def _(pool):
            nc.gpsimd.memset(zero[:], 0.0).then_inc(zeroed, 1)
            nc.gpsimd.memset(v_pad[:], 0.0).then_inc(prep_pool, 1)
            nc.gpsimd.memset(ones_bf[:], 1.0).then_inc(prep_pool, 1)
            nc.gpsimd.memset(r_acc[:], 0.0).then_inc(prep_pool, 1)
            pool.wait_ge(d_cst, 16)
            pool.wait_ge(vars_ready, 1)
            nc.gpsimd.tensor_tensor(rstd_x[:], ve_x[:], cst[:, C_POW:C_POW + NB], ALU.pow).then_inc(rstd_ready, 1)

            def spare_pool(n):
                nc.gpsimd.tensor_tensor(tiny[:, n:n + 1], cst[:, C_POW:C_POW + 1], cst[:, C_POW:C_POW + 1], ALU.mult)

            def norm(batch, k, rec, p_buf, rec_s, norm_s):
                rec_s.wait(pool, batch, k + 1)
                nc.gpsimd.tensor_tensor(p_buf[:, k % 2], p_buf[:, k % 2],
                                        rec[:, HC * k:HC * k + HC].unsqueeze(2).broadcast_to([P, HC, P]),
                                        ALU.mult).then_inc(norm_s.sem, 1)

            def rstd(batch, n, var_s, ve, rs, rstd_s):
                var_s.wait(pool, batch, n + 1)
                nc.gpsimd.tensor_tensor(rs[:, n:n + 1], ve[:, n:n + 1], cst[:, C_POW:C_POW + 1],
                                        ALU.pow).then_inc(rstd_s.sem, 1)

            def body(a, b, c):
                if c is not None:
                    if later(c):
                        d_scatter.wait(pool, c - 1)
                    h2n_ready.wait(pool, c, carrier=lambda: spare_pool(1))
                    nc.gpsimd.tensor_copy(h2s[:], h2n[:]).then_inc(h2s_ready.sem, 1)
                for k in range(CHUNKS):
                    if a is not None:
                        norm(a, k, rec_a, p_a, a_rec, a_norm)
                    if b is not None:
                        norm(b, k, rec_b, p_b, b_rec, b_norm)
                if b is not None:
                    rstd(b, 0, b_var, ve_b, rs_b, b_rstd)
                if a is not None:
                    rstd(a, 0, a_var, ve_a, rs_a, a_rstd)
                    rstd(a, 1, a_var, ve_a, rs_a, a_rstd)
                if c is not None:
                    if isinstance(c, int) and c == 0:
                        pool.wait_ge(d_zero, 16 * NE * CAP // 512)
                    slots_ready.wait(pool, c)
                    h2s_ready.wait(pool, c, carrier=lambda: spare_pool(2))
                    for k in range(TOPK):
                        pool.indirect_dma_start(out=queue_in, out_offset=bass.IndirectOffsetOnAxis(ap=r_slot[:, k:k + 1], axis=0),
                                                in_=h2s[:], in_offset=None).then_inc(d_scatter.sem, 16)
            batches(pool, body)
            for half in range(2):
                d_eo[half].wait(pool, NE // 2 - 1)
            for n in range(NB):
                for k in range(TOPK):
                    pool.indirect_dma_start(out=got[:, n, k, :], out_offset=None, in_=queue_out,
                                            in_offset=bass.IndirectOffsetOnAxis(ap=from_all[:, n, k:k + 1], axis=0)
                                            ).then_inc(d_got[n].sem, 16)

        @block.scalar
        def _(act):
            act.dma_start(cst[:], const).then_inc(d_cst, 16)
            for n, v in enumerate((ln1_g, ln1_b, ln2_g, ln2_b)):
                act.dma_start(rows[n:n + 1, :], v.rearrange("(o d) -> o d", o=1)).then_inc(d_rows, 16)
            act.dma_start(rows[4:NV, :], b1.rearrange("e (m p) -> (e m) p", p=P)).then_inc(d_rows, 16)
            act.dma_start(gates2[:, 0:1], g_x.partition_broadcast(P)).then_inc(d_small, 16)
            act.dma_start(gates2[:, 1:2], g_f.partition_broadcast(P)).then_inc(d_small, 16)
            act.dma_start(bo_bc[:], bo.partition_broadcast(P)).then_inc(d_small, 16)
            act.dma_start(wproj_sb[:], wproj).then_inc(d_small, 16)
            act.dma_start(wgate_sb[:], wgate).then_inc(d_small, 16)
            act.dma_start(mask_i32[:], mask.rearrange("(o b) t -> o (b t)", o=1).partition_broadcast(P)).then_inc(d_mask, 16)
            act.wait_ge(d_small, 80)
            nc.scalar.activation(tanh2[:], gates2[:], ACT.Tanh).then_inc(tanh_ready, 1)

            def turn_xc(a):
                xc_turned.wait(act, a)
                nc.scalar.copy(xcT[:], b_misc[:, 0:2 * P]).then_inc(xcT_ready.sem, 1)

            def exps(batch, k, bank_, nmax, sums, p_buf, max_s, turned_s, exp_s):
                max_s.wait(act, batch, k + 1)
                if k >= 2:
                    turned_s.wait(act, batch, k - 1)
                elif later(batch):
                    turned_s.wait(act, batch - 1, CHUNKS + k - 1)
                for j in range(HC):
                    n = HC * k + j
                    last = nc.scalar.activation(p_buf[:, k % 2, j, :], bank_[:, j * P:(j + 1) * P], ACT.Exp,
                                                bias=nmax[:, n:n + 1], accum_out=sums[:, n:n + 1])
                last.then_inc(exp_s.sem, 1)

            turn_xc(0)

            def body(a, b, c):
                if a is not None:
                    for f in range(2):
                        q_made.wait(act, a, f + 1)
                        nc.scalar.mul(qT[:, 4 * f:4 * f + 4, :].rearrange("p m t -> p (m t)"), q_banks[f][:],
                                      float(XD) ** -0.5).then_inc(q_ready.sem, 1)
                    v_made.wait(act, a, 1)
                    nc.scalar.copy(v_sb[:, 0:512], v_banks[0][:]).then_inc(v_ready0.sem, 1)
                for k in range(CHUNKS + LAG):
                    if a is not None and k < CHUNKS:
                        exps(a, k, s_a, nmax_a, sum_a, p_a, a_max, a_turned, a_exp)
                    if a is not None and k == 1 and has_next(a):
                        turn_xc(a + 1)
                    if b is not None and k >= LAG:
                        b_turned.wait(act, b, k - LAG + 1)
                        nc.scalar.copy(pT_b[:].rearrange("p h t -> p (h t)"), t_b[:]).then_inc(b_pT.sem, 1)
                    if b is not None and k < CHUNKS:
                        exps(b, k, s_b, nmax_b, sum_b, p_b, b_max, b_turned, b_exp)
                    if c is not None and k == 2:
                        lmax_ready.wait(act, c)
                        nc.scalar.activation(r_exp[:], c_bank[:, P:P + NE], ACT.Exp, bias=r_nmax[:],
                                             accum_out=r_sum[:]).then_inc(lexp_ready.sem, 1)
            batches(act, body)
            for e in range(NE):
                for m in range(MT):
                    h_made.wait(act, e, m // 2 + 1)
                    if m == 0 and e >= 2:
                        e_made.wait(act, e - 2)
                    hb = bk[1 + 2 * (e % 2) + m // 2]
                    nc.scalar.activation(hid[:, e % 2, m, :], hb[:, (m % 2) * 256:(m % 2) * 256 + 256], ACT.Gelu,
                                         bias=cols[:, 4 + e * MT + m:5 + e * MT + m]).then_inc(h_act.sem, 1)
                eo_ready.wait(act, e)
                act.dma_start(queue_out[e * CAP:(e + 1) * CAP, :].rearrange("(t p) d -> p t d", p=P),
                              eo[:, e % 2, :, :]).then_inc(d_eo[e % 2].sem, 16)

        @block.vector
        def _(dve):
            n_prep = [0]

            def link(ins):
                n_prep[0] += 1
                ins.then_inc(prep, 1)
                dve.wait_ge(prep, n_prep[0])

            dve.wait_ge(d_x, 16)
            for n in range(NB):
                last = nc.vector.bn_stats(stats_x[:, n, :], x_all[:, n, :])
            link(last)
            for n in range(NB):
                last = nc.vector.bn_aggr(mv_x[:, n, :], stats_x[:, n, :])
            link(last)
            nc.vector.tensor_scalar(ve_x[:], mv_x[:, :, 1], EPS, None, ALU.add).then_inc(vars_ready, 1)
            dve.wait_ge(d_cst, 16)
            nc.vector.tensor_copy(ident_bf[:], ident)
            nc.vector.tensor_copy(tri_bf[:], cst[:, C_TRI:C_TRI + P])
            link(nc.vector.tensor_copy(causal_bf[:], cst[:, C_CAUSAL:C_CAUSAL + P]))

            def apply_xn(a):
                nc.vector.tensor_scalar(xn[:], x_all[:, a, :], mv_x[:, a, 0:1], rstd_x[:, bass.ds(a, 1)],
                                        ALU.subtract, ALU.mult).then_inc(xn_ready.sem, 1)
            dve.wait_ge(rstd_ready, 1)
            apply_xn(0)
            dve.wait_ge(d_mask, 16)
            link(nc.vector.tensor_scalar(mask_neg[:], mask_i32[:], NEG, None, ALU.mult))
            nc.vector.tensor_tensor(mask_all[:].rearrange("p (b t) -> p b t", b=NB),
                                    mask_neg[:].rearrange("p (b t) -> p b t", b=NB),
                                    causal_bf[:].unsqueeze(1).broadcast_to([P, NB, P]), ALU.min).then_inc(consts_ready, 1)
            dve.wait_ge(rows_turned, 1)
            nc.vector.tensor_copy(cols[:], c_bank[:, 0:NV]).then_inc(cols_ready, 1)
            dve.wait_ge(d_wqkv, 16)
            src = wqkv_sb[:].rearrange("p (h s d) -> p s h d", h=SH, s=3)
            for s in range(2):
                dst = w4_sb[:, s, :].rearrange("p (h d) -> p h d", h=SH)
                rot = w4_sb[:, 2 + s, :].rearrange("p (h d) -> p h d", h=SH)
                nc.vector.tensor_copy(dst, src[:, s])
                nc.vector.tensor_scalar(rot[:, :, 0:SD // 2], src[:, s, :, SD // 2:SD], -1.0, None, ALU.mult)
                nc.vector.tensor_copy(rot[:, :, SD // 2:SD], src[:, s, :, 0:SD // 2])
            nc.vector.tensor_copy(wvs_sb[:].rearrange("p (h d) -> p h d", h=SH), src[:, 2]).then_inc(w4_ready, 1)
            dve.wait_ge(tanh_ready, 1)
            link(nc.vector.tensor_scalar(bo_bc[:], bo_bc[:], tanh2[:, 0:1], None, ALU.mult))
            nc.vector.tensor_tensor(x1_all[:], x_all[:], bo_bc[:].unsqueeze(1).broadcast_to([P, NB, P]),
                                    ALU.add).then_inc(xb_ready, 1)
            dve.wait_ge(xb_ready, 1)
            dve.wait_ge(prep_pool, 3)
            dve.wait_ge(cols_ready, 1)

            def spare_dve():
                nc.vector.memset(tiny[:, 0:1], 0.0)

            a_links, b_links, c_links = Chain(dve, a_chain), Chain(dve, b_chain), Chain(dve, c_chain)

            def row_max(batch, k, bank_, nmax, scores_s, max_s):
                scores_s.wait(dve, batch, k + 1)
                nc.vector.tensor_reduce(nmax[:, HC * k:HC * k + HC], bank_[:].rearrange("p (h t) -> p h t", h=HC),
                                        AX.X, ALU.max, negate=True).then_inc(max_s.sem, 1)

            def recip(batch, k, sums, rec, exp_s, rec_s):
                exp_s.wait(dve, batch, k + 1)
                nc.vector.reciprocal(rec[:, HC * k:HC * k + HC], sums[:, HC * k:HC * k + HC]).then_inc(rec_s.sem, 1)

            def body(a, b, c):
                if a is not None:
                    for f in range(2):
                        k_made.wait(dve, a, f + 1)
                        nc.vector.tensor_copy(kT[:, 4 * f:4 * f + 4, :].rearrange("p m t -> p (m t)"),
                                              k_banks[f][:]).then_inc(k_ready.sem, 1)
                    v_made.wait(dve, a, 2)
                    nc.vector.tensor_copy(v_sb[:, 512:1024], v_banks[1][:]).then_inc(v_ready1.sem, 1)
                if b is not None:
                    h_turned.wait(dve, b)
                    nc.vector.tensor_scalar(hT[:], b_misc[:, 0:P], cols[:, 0:1], cols[:, 1:2],
                                            ALU.mult, ALU.add).then_inc(hT_ready.sem, 1)
                    b_links.start(b)
                    qk_made.wait(dve, b)
                    nc.vector.tensor_tensor(rope1[:], o_a[:, 0:2 * P], cos_qk, ALU.mult)
                    nc.vector.tensor_tensor(rope2[:], o_a[:, 2 * P:4 * P], sin_qk, ALU.mult).then_inc(qk_read.sem, 1)
                    qk_read.wait(dve, b)
                    b_links.link(nc.vector.tensor_tensor(qk[:].rearrange("p s t -> p (s t)"), rope1[:], rope2[:], ALU.add))
                    for j in range(HC):
                        last = nc.vector.tensor_scalar(km[:, j, :], qk[:, 1, :], cst[:, C_HMASK + j:C_HMASK + j + 1],
                                                       None, ALU.mult)
                    last.then_inc(qkm_ready.sem, 1)
                    vs_made.wait(dve, b)
                    nc.vector.tensor_copy(
                        v_diag, b_misc[:, 0:P].rearrange("p (g j d) -> p g j d", g=4, j=HC)).then_inc(vs_ready.sem, 1)
                if a is not None and has_next(a):
                    apply_xn(a + 1)
                for k in range(CHUNKS + LAG):
                    if a is not None and 1 <= k <= CHUNKS:
                        recip(a, k - 1, sum_a, rec_a, a_exp, a_rec)
                    if a is not None and k >= LAG:
                        a_turned.wait(dve, a, k - LAG + 1)
                        nc.vector.tensor_copy(pT_a[:].rearrange("p h t -> p (h t)"), t_a[:]).then_inc(a_pT.sem, 1)
                    if a is not None and k < CHUNKS:
                        row_max(a, k, s_a, nmax_a, a_scores, a_max)
                    if b is not None and 1 <= k <= CHUNKS:
                        recip(b, k - 1, sum_b, rec_b, b_exp, b_rec)
                    if b is not None and k < CHUNKS:
                        row_max(b, k, s_b, nmax_b, b_scores, b_max)
                    if a is not None and k - LAG in (1, 3):
                        a_pv.wait(dve, a, k - LAG + 1)
                        nc.vector.tensor_copy(oT_a[:].rearrange("p m t -> p (m t)"), o_a[:]).then_inc(a_oT.sem, 1)
                    if c is not None:
                        route(c, k)
                if b is not None:
                    b_pv.wait(dve, b)
                    nc.vector.tensor_copy(oT_b[:], b_misc[:, 0:P]).then_inc(b_oT.sem, 1)
                if a is not None:
                    a_links.start(a)
                    a_y.wait(dve, a)
                    nc.vector.scalar_tensor_tensor(out=x1_all[:, a, :], in0=y_bank[:, 0:P], scalar=tanh2[:, 0:1],
                                                   in1=x1_all[:, a, :], op0=ALU.mult, op1=ALU.add).then_inc(a_x1.sem, 1)
                    a_x1.wait(dve, a, carrier=spare_dve)
                    a_links.link(nc.vector.bn_stats(st_a[:, 0, :], x1_all[:, a, :]), spare_dve)
                    a_links.link(nc.vector.bn_aggr(mv_a[:, 0, :], st_a[:, 0, :]))
                    nc.vector.tensor_scalar(ve_a[:, 0:1], mv_a[:, 0, 1:2], EPS, None, ALU.add).then_inc(a_var.sem, 1)
                if b is not None:
                    b_proj.wait(dve, b)
                    b_links.link(nc.vector.tensor_tensor(z_all[:, b, :], b_misc[:, 2 * P:3 * P], z_all[:, b, :], ALU.add), spare_dve)
                    b_links.link(nc.vector.bn_stats(st_b[:], z_all[:, b, :]), spare_dve)
                    b_links.link(nc.vector.bn_aggr(mv_b[:], st_b[:]))
                    nc.vector.tensor_scalar(ve_b[:], mv_b[:, 1:2], EPS, None, ALU.add).then_inc(b_var.sem, 1)
                    b_links.end()
                if a is not None:
                    a_rstd.wait(dve, a, 1)
                    a_links.link(nc.vector.tensor_scalar(z_all[:, a, :], x1_all[:, a, :], mv_a[:, 0, 0:1], rs_a[:, 0:1],
                                                         ALU.subtract, ALU.mult), spare_dve)
                    a_links.link(nc.vector.bn_stats(st_a[:, 1, :], z_all[:, a, :]), spare_dve)
                    a_links.link(nc.vector.bn_aggr(mv_a[:, 1, :], st_a[:, 1, :]))
                    nc.vector.tensor_scalar(ve_a[:, 1:2], mv_a[:, 1, 1:2], EPS, None, ALU.add).then_inc(a_var.sem, 1)
                if b is not None:
                    b_rstd.wait(dve, b)
                    nc.vector.tensor_scalar(h2n[:], z_all[:, b, :], mv_b[:, 0:1], rs_b[:, 0:1],
                                            ALU.subtract, ALU.mult).then_inc(h2n_ready.sem, 1)
                if a is not None:
                    a_rstd.wait(dve, a, 2)
                    nc.vector.tensor_scalar(h_sb[:], z_all[:, a, :], mv_a[:, 1, 0:1], rs_a[:, 1:2],
                                            ALU.subtract, ALU.mult).then_inc(h_ready.sem, 1)
                    a_links.end()

            v_diag = v_pad[:].rearrange("p (g j) c -> p g (j c)", g=4)
            v_diag = bass.AP(tensor=v_diag.tensor, offset=v_diag.offset,
                             ap=[list(v_diag.ap[0]), [HC * HC * SD, 4], [HC * SD + SD, HC], [1, SD]])

            def route(c, k):
                if k == 1:
                    h2_turned.wait(dve, c)
                    nc.vector.tensor_scalar(h2T[:], c_bank[:, 0:P], cols[:, 2:3], cols[:, 3:4],
                                            ALU.mult, ALU.add).then_inc(h2T_ready.sem, 1)
                if k == 2:
                    logits_made.wait(dve, c)
                    nc.vector.tensor_reduce(r_nmax[:], c_bank[:, P:P + NE], AX.X, ALU.max, negate=True).then_inc(lmax_ready.sem, 1)
                if k == 3:
                    c_links.start(c)
                    lexp_ready.wait(dve, c)
                    c_links.link(nc.vector.reciprocal(r_rec[:], r_sum[:]))
                    c_links.link(nc.vector.tensor_scalar(r_gate[:], r_exp[:], r_rec[:, 0:1], None, ALU.mult), spare_dve)
                    c_links.link(nc.vector.max(r_top[:], r_gate[:]), spare_dve)
                    c_links.link(nc.vector.max_index(r_idx[:], r_top[:], r_gate[:]))
                    c_links.link(nc.vector.tensor_copy(r_idxf[:], r_idx[:, 0:TOPK]))
                    c_links.link(nc.vector.tensor_tensor(r_mk[:], iota2, r_idxf[:].unsqueeze(2).broadcast_to([P, TOPK, NE]),
                                                         ALU.is_equal))
                    nc.vector.tensor_tensor(r_mask[:], r_mk[:, 0, :], r_mk[:, 1, :], ALU.add).then_inc(choice_ready.sem, 1)
                if k == 5:
                    pos_made.wait(dve, c)
                    nc.vector.tensor_tensor(r_pm[:], r_mk[:], c_bank[:, 256:256 + NE].unsqueeze(1).broadcast_to([P, TOPK, NE]),
                                            ALU.mult).then_inc(pos_read.sem, 1)
                    pos_read.wait(dve, c)
                    nc.vector.tensor_tensor(r_acc[:], r_acc[:], r_mask[:], ALU.add)
                    c_links.link(nc.vector.tensor_reduce(r_pos[:], r_pm[:], AX.X, ALU.add))
                    nc.vector.scalar_tensor_tensor(out=gate_all[:, c, :], in0=r_pos[:], scalar=float(CAP),
                                                   in1=r_top[:, 0:TOPK], op0=ALU.is_le, op1=ALU.mult)
                    nc.vector.tensor_scalar(r_keep[:], r_pos[:], float(CAP), None, ALU.is_le)
                    nc.vector.scalar_tensor_tensor(out=r_drop[:], in0=r_pos[:], scalar=float(CAP),
                                                   in1=cst_trash(c), op0=ALU.is_gt, op1=ALU.mult)
                    c_links.link(nc.vector.tensor_scalar(r_pmin[:], r_pos[:], float(CAP), -1.0, ALU.min, ALU.add))
                    c_links.link(nc.vector.scalar_tensor_tensor(out=r_row[:], in0=r_idxf[:], scalar=float(CAP), in1=r_pmin[:],
                                                                op0=ALU.mult, op1=ALU.add))
                    c_links.link(nc.vector.tensor_copy(from_all[:, c, :], r_row[:]))
                    c_links.link(nc.vector.tensor_tensor(r_kept[:], r_row[:], r_keep[:], ALU.mult))
                    c_links.link(nc.vector.tensor_tensor(r_row[:], r_kept[:], r_drop[:], ALU.add))
                    if later(c):
                        d_scatter.wait(dve, c - 1)
                    nc.vector.tensor_copy(r_slot[:], r_row[:]).then_inc(slots_ready.sem, 1)
                    c_links.end()

            trash = cst[:, C_TRASH:C_TRASH + 2 * NB].rearrange("p (b k) -> p b k", k=TOPK)

            def cst_trash(c):
                return trash[:, c, :]

            batches(dve, body)

            dve.wait_ge(d_b2, 16)
            for e in range(NE):
                def turn(e):
                    x_turned.wait(dve, e)
                    nc.vector.tensor_scalar(xT[:, e % 2, :], bk[0][:, 0:2 * P], cols[:, 2:3], cols[:, 3:4],
                                            ALU.mult, ALU.add).then_inc(xT_ready.sem, 1)
                if e == 0:
                    turn(0)
                if e + 1 < NE:
                    turn(e + 1)
                e_made.wait(dve, e)
                if e >= 2:
                    d_eo[e % 2].wait(dve, e // 2 - 1)
                nc.vector.tensor_tensor(eo[:, e % 2, :, :], bk[5 + e % 2][:, 0:2 * P].rearrange("p (t d) -> p t d", t=2),
                                        b2_bc[:, e, :].unsqueeze(1).broadcast_to([P, 2, P]), ALU.add).then_inc(eo_ready.sem, 1)
            mix = Chain(dve, mix_chain)
            for n in range(NB):
                d_got[n].wait(dve, 0)
                mix.start(n)
                mix.link(nc.vector.scalar_tensor_tensor(out=acc[:, 0, :], in0=got[:, n, 0, :], scalar=gate_all[:, n, 0:1],
                                                        in1=z_all[:, n, :], op0=ALU.mult, op1=ALU.add))
                mix.link(nc.vector.scalar_tensor_tensor(out=acc[:, 1, :], in0=got[:, n, 1, :], scalar=gate_all[:, n, 1:2],
                                                        in1=acc[:, 0, :], op0=ALU.mult, op1=ALU.add))
                nc.vector.scalar_tensor_tensor(out=res[:, n, :], in0=acc[:, 1, :], scalar=tanh2[:, 1:2],
                                               in1=x1_all[:, n, :], op0=ALU.mult, op1=ALU.add).then_inc(mixed.sem, 1)

        @block.tensor
        def _(pe):
            def turn_xc(a):
                xn_ready.wait(pe, a)
                d_ctx.wait(pe, a)
                nc.tensor.transpose(b_misc[:, 0:P], xn[:], ident)
                nc.tensor.transpose(b_misc[:, P:2 * P], c_sb[:], ident).then_inc(xc_turned.sem, 1)

            pe.wait_ge(d_cst, 16)
            pe.wait_ge(d_rows, 80)
            nc.tensor.transpose(c_bank[:, 0:NV], rows[:], ident[0:NV, 0:NV]).then_inc(rows_turned, 1)
            turn_xc(0)
            pe.wait_ge(consts_ready, 1)
            pe.wait_ge(cols_ready, 1)

            def project(a):
                xcT_ready.wait(pe, a)
                if isinstance(a, int) and a == 0:
                    pe.wait_ge(d_wq, 16)
                    pe.wait_ge(d_wk, 16)
                    pe.wait_ge(d_wv, 16)
                for w, half, banks, made in ((wq_sb, xcT[:, 0:P], q_banks, q_made), (wk_sb, xcT[:, P:2 * P], k_banks, k_made)):
                    for f in range(2):
                        if later(a):
                            if f == 0:
                                (a_exp if w is wq_sb else a_pT).wait(pe, a - 1)
                            elif not isinstance(a, int) or a >= 2:
                                (b_exp if w is wq_sb else b_pT).wait(pe, a - 2)
                        for m in range(4):
                            last = nc.tensor.matmul(banks[f][:, m * P:(m + 1) * P], w[:, (4 * f + m) * P:(4 * f + m + 1) * P],
                                                    half, start=True, stop=True)
                        last.then_inc(made.sem, 1)
                for f in range(2):
                    if f == 0 and (not isinstance(a, int) or a >= 3):
                        pos_read.wait(pe, a - 3)
                    if f == 1 and later(a):
                        a_x1.wait(pe, a - 1)
                    nc.tensor.matmul(v_banks[f][:], xcT[:, P:2 * P], wv_sb[:, f * 512:(f + 1) * 512],
                                     start=True, stop=True).then_inc(v_made.sem, 1)

            def project_b(b):
                h_ready.wait(pe, b)
                if later(b):
                    h2n_free(b)
                nc.tensor.transpose(b_misc[:, 0:P], h_sb[:], ident).then_inc(h_turned.sem, 1)
                hT_ready.wait(pe, b)
                if isinstance(b, int) and b == 0:
                    pe.wait_ge(w4_ready, 1)
                a_oT.wait(pe, b)
                for s in range(4):
                    last = nc.tensor.matmul(o_a[:, s * P:(s + 1) * P], w4_sb[:, s, :], hT[:], start=True, stop=True)
                last.then_inc(qk_made.sem, 1)
                nc.tensor.matmul(b_misc[:, 0:P], hT[:], wvs_sb[:], start=True, stop=True).then_inc(vs_made.sem, 1)

            def h2n_free(b):
                h2n_ready.wait(pe, b - 1)

            def scores_a(a, k):
                r = XD * (k % 2)
                if k == 0:
                    q_ready.wait(pe, a)
                    k_ready.wait(pe, a)
                else:
                    a_exp.wait(pe, a, k)
                nc.tensor.matmul(s_a[:], ident_bf[:], mask_all[:, bass.ts(a, P)].unsqueeze(1).broadcast_to([P, HC, P]),
                                 start=True, stop=False, skip_group_check=True)
                for j in range(HC):
                    m = 4 * (k // 2) + j
                    last = nc.tensor.matmul(s_a[:, j * P:(j + 1) * P], qT[r:r + XD, m, :], kT[r:r + XD, m, :],
                                            start=False, stop=True, skip_group_check=True)
                last.then_inc(a_scores.sem, 1)

            def scores_b(b, k):
                if k == 0:
                    qkm_ready.wait(pe, b)
                    if has_next(b):
                        q_ready.wait(pe, b + 1, 2)
                else:
                    b_exp.wait(pe, b, k)
                nc.tensor.matmul(s_b[:], ident_bf[:], causal_bf[:].unsqueeze(1).broadcast_to([P, HC, P]),
                                 start=True, stop=False, skip_group_check=True)
                r = 32 * k
                nc.tensor.matmul(s_b[:], qk[r:r + 32, 0, :], km[r:r + 32, :, :].rearrange("p h t -> p (h t)"),
                                 start=False, stop=True, skip_group_check=True, tile_position=(r, 0)).then_inc(b_scores.sem, 1)

            def turn_p(batch, k, bank_, p_buf, norm_s, pT_s, turned_s):
                norm_s.wait(pe, batch, k + 1)
                if k >= 1:
                    pT_s.wait(pe, batch, k)
                for j in range(HC):
                    last = nc.tensor.transpose(bank_[:, j * P:(j + 1) * P], p_buf[:, k % 2, j, :], ident)
                last.then_inc(turned_s.sem, 1)

            def pv_a(a, k):
                r = XD * (k % 2)
                a_pT.wait(pe, a, k + 1)
                if k == 0:
                    v_ready0.wait(pe, a)
                    v_ready1.wait(pe, a)
                    if a is not None and not (isinstance(a, int) and a == 0):
                        qk_read.wait(pe, a - 1)
                if k == 2:
                    a_oT.wait(pe, a, 1)
                for j in range(HC):
                    h = 8 * (k // 2) + 2 * j + k % 2
                    last = nc.tensor.matmul(o_a[r:r + XD, j * P:(j + 1) * P], v_sb[:, h * XD:(h + 1) * XD], pT_a[:, j, :],
                                            start=True, stop=True)
                last.then_inc(a_pv.sem, 1)

            def pv_b(b, g):
                b_pT.wait(pe, b, g + 1)
                if g == 0:
                    vs_ready.wait(pe, b)
                    if has_next(b) and not (isinstance(b, int) and b + 2 >= NB):
                        xcT_ready.wait(pe, b + 2)
                for j in range(HC):
                    last = nc.tensor.matmul(b_misc[32 * g:32 * g + 32, 0:P], v_pad[:, HC * g + j, :], pT_b[:, j, :],
                                            start=(j == 0), stop=(j == HC - 1))
                if g == CHUNKS - 1:
                    last.then_inc(b_pv.sem, 1)

            def output_a(a, half):
                a_oT.wait(pe, a, half + 1)
                if isinstance(a, int) and a == 0:
                    pe.wait_ge(d_wo, 16)
                for m in range(4):
                    last = nc.tensor.matmul(y_bank[:, 0:P], oT_a[:, m, :], wo_sb[:, 4 * half + m, :],
                                            start=(half == 0 and m == 0), stop=(half == 1 and m == 3))
                if half == 1:
                    last.then_inc(a_y.sem, 1)

            def body(a, b, c):
                if a is not None:
                    project(a)
                if b is not None:
                    project_b(b)
                for k in range(CHUNKS + LAG):
                    t = k - LAG
                    if a is not None and t >= 0:
                        turn_p(a, t, t_a, p_a, a_norm, a_pT, a_turned)
                    if a is not None and k < CHUNKS:
                        scores_a(a, k)
                    if c is not None and k == 0:
                        h2n_ready.wait(pe, c)
                        if has_next(c) and not (isinstance(c, int) and c + 2 >= NB):
                            v_ready0.wait(pe, c + 2)
                        nc.tensor.transpose(c_bank[:, 0:P], h2n[:], ident).then_inc(h2_turned.sem, 1)
                    if b is not None and t >= 0:
                        turn_p(b, t, t_b, p_b, b_norm, b_pT, b_turned)
                    if a is not None and t >= 0:
                        pv_a(a, t)
                    if b is not None and k < CHUNKS:
                        scores_b(b, k)
                    if b is not None and t >= 0:
                        pv_b(b, t)
                    if a is not None and k == 1 and has_next(a):
                        if b is not None:
                            vs_ready.wait(pe, b)
                        turn_xc(a + 1)
                    if c is not None and k == 1:
                        h2T_ready.wait(pe, c)
                        nc.tensor.matmul(c_bank[:, P:P + NE], h2T[:], wgate_sb[:], start=True, stop=True).then_inc(logits_made.sem, 1)
                    if c is not None and k == 3:
                        choice_ready.wait(pe, c)
                        nc.tensor.matmul(c_bank[:, 256:256 + NE], tri_bf[:], r_mask[:], start=True, stop=False)
                        nc.tensor.matmul(c_bank[:, 256:256 + NE], ones_bf[:], r_acc[:], start=False, stop=True).then_inc(pos_made.sem, 1)
                    if a is not None and k == 4:
                        output_a(a, 0)
                if a is not None:
                    output_a(a, 1)
                if b is not None:
                    b_oT.wait(pe, b)
                    nc.tensor.matmul(b_misc[:, 2 * P:3 * P], oT_b[:], wproj_sb[:], start=True, stop=True).then_inc(b_proj.sem, 1)
            batches(pe, body)

            def turn_x(e):
                d_xin[e % RING].wait(pe, e // RING)
                if e >= 1:
                    xT_ready.wait(pe, e - 1)
                for t in range(2):
                    last = nc.tensor.transpose(bk[0][:, t * P:(t + 1) * P], xin[:, e % RING, t, :], ident)
                last.then_inc(x_turned.sem, 1)

            def hidden(e):
                xT_ready.wait(pe, e)
                d_w[e % RING].wait(pe, e // RING)
                if e >= 2:
                    h_act.wait(pe, e - 2)
                for m in range(MT):
                    last = nc.tensor.matmul(bk[1 + 2 * (e % 2) + m // 2][:, (m % 2) * 256:(m % 2) * 256 + 256],
                                            w1_sb[:, e % RING, m * P:(m + 1) * P], xT[:, e % 2, :], start=True, stop=True)
                    if m % 2:
                        last.then_inc(h_made.sem, 1)

            def expert_out(e):
                h_act.wait(pe, e)
                if e >= 2:
                    eo_ready.wait(pe, e - 2)
                for t in range(2):
                    for m in range(MT):
                        last = nc.tensor.matmul(bk[5 + e % 2][:, t * P:(t + 1) * P], hid[:, e % 2, m, t * P:(t + 1) * P],
                                                w2_sb[:, e % RING, m, :], start=(m == 0), stop=(m == MT - 1))
                last.then_inc(e_made.sem, 1)

            turn_x(0)
            for e in range(NE):
                hidden(e)
                if e + 1 < NE:
                    turn_x(e + 1)
                if e >= 1:
                    expert_out(e - 1)
            expert_out(NE - 1)


def constants():
    import numpy as np
    c = np.zeros((P, NCONST), np.float32)
    p, t = np.arange(P)[:, None], np.arange(P)[None, :]
    c[:, C_ID:C_ID + P] = p == t
    c[:, C_CAUSAL:C_CAUSAL + P] = np.where(t > p, np.float32(NEG), np.float32(0))
    c[:, C_TRI:C_TRI + P] = p <= t
    freq = (np.float32(1) / np.float32(10000) ** (np.arange(0, SD, 2, dtype=np.float32) / np.float32(SD))).astype(np.float32)
    angle = freq[np.arange(P) % (SD // 2)][:, None] * np.arange(P, dtype=np.float32)[None, :]
    for at, f in ((C_COS, np.cos), (C_SIN, np.sin)):
        c[:, at:at + P] = f(angle) * np.float32(SD ** -0.5)
        c[:, at + P:at + 2 * P] = f(angle)
    c[:, C_HMASK:C_HMASK + HC] = (p // SD) % HC == np.arange(HC)[None, :]
    c[:, C_IOTA:C_IOTA + 2 * NE] = np.tile(np.arange(NE), 2)[None, :]
    c[:, C_TRASH:C_TRASH + 2 * NB] = NE * CAP + np.arange(2 * NB)[None, :] * P + p
    c[:, C_POW:C_POW + NB] = -0.5
    return c


_INS = ['x', 'ctx_1024', 'mask_BxS2_bf0', 'g_xattn', 'g_ffn', 'L0_xattn_Wq', 'L0_xattn_Wk', 'L0_xattn_Wv', 'L0_xattn_Wo',
        'L0_xattn_bo', 'L0_ffn_ln1_g', 'L0_ffn_ln1_b', 'L0_ffn_Wqkv', 'L0_ffn_Wproj', 'L0_ffn_ln2_g', 'L0_ffn_ln2_b',
        'L0_ffn_Wgate', 'L0_ffn_W1', 'L0_ffn_b1', 'L0_ffn_W2', 'L0_ffn_b2']


def kernel(**inputs):
    import numpy as _np
    import concourse.bacc as _bacc
    from concourse import mybir as _mybir
    from concourse.bass_utils import run_bass_kernel_spmd as _run

    nc = _bacc.Bacc("TRN2", target_bir_lowering=False, num_devices=1)
    arrays, args = {}, []
    for name in _INS:
        a = _np.ascontiguousarray(inputs[name])
        if a.dtype.kind == "b":
            a = a.astype(_np.int32)
        arrays[f"in_{name}"] = a
    arrays["in_const"] = constants()
    for name, a in arrays.items():
        args.append(nc.dram_tensor(name, a.shape, _mybir.dt.from_np(a.dtype), kind="ExternalInput").ap())
    args.append(nc.dram_tensor("out_0", (NB, P, P), _mybir.dt.float32, kind="ExternalOutput").ap())
    build(nc, *args)
    r = _run(nc, [arrays], core_ids=[0])
    return r.results[0]["out_0"]
```

```python
from contextlib import ExitStack

import concourse.bass as bass
from concourse import mybir

F32 = mybir.dt.float32
BF16 = mybir.dt.bfloat16
U32 = mybir.dt.uint32
I32 = mybir.dt.int32
ALU = mybir.AluOpType
ACT = mybir.ActivationFunctionType
AX = mybir.AxisListType

P = 128
NB = 8
XH, XD = 16, 64
INNER = XH * XD
SH, SD = 16, 8
NE, FF = 8, 512
TOPK = 2
CAP = 2 * NB * P // NE
CHUNKS, HC = 4, 4
EPS = 1e-5
NEG = -(2.0 - 2.0 ** -7) * 2.0 ** 127
RING = 4
MT = FF // P

C_ID, C_CAUSAL, C_TRI = 0, P, 2 * P
C_COS = 3 * P
C_SIN = C_COS + 2 * P
C_HMASK = C_SIN + 2 * P
C_IOTA = C_HMASK + HC
C_TRASH = C_IOTA + 2 * NE
C_POW = C_TRASH + 2 * NB
NCONST = C_POW + NB

LOOP = True


class Signal:

    def __init__(self, sem, per):
        self.sem, self.per = sem, per

    def wait(self, eng, batch, k=None, carrier=None):
        eng.wait_ge(self.sem, batch * self.per + (self.per if k is None else k))
        if carrier is not None and not isinstance(batch, int):
            carrier()


class Chain:

    def __init__(self, eng, rises):
        self.eng, self.rises, self.n = eng, rises, 0

    def start(self, batch):
        self.batch, self.n = batch, 0

    def link(self, ins, carrier=None):
        self.n += 1
        ins.then_inc(self.rises.sem, 1)
        self.rises.wait(self.eng, self.batch, self.n, carrier)

    def end(self):
        assert self.n == self.rises.per, (self.n, self.rises.per)


def build(nc, x, ctx_in, mask, g_x, g_f, wq, wk, wv, wo, bo, ln1_g, ln1_b, wqkv, wproj, ln2_g, ln2_b,
          wgate, w1, b1, w2, b2, const, out):
    stack = ExitStack()
    with stack:
        def sb(name, shape, dt=F32):
            return stack.enter_context(nc.sbuf_tensor(name, shape, dt))

        def bank(name):
            return stack.enter_context(nc.psum_tensor(name, [P, 512], F32))

        def sem(name):
            return stack.enter_context(nc.semaphore(name))

        def signal(name, per):
            return Signal(sem(name), per)

        queue_in = nc.dram_tensor("queue_in", [NE * CAP + NB * P * TOPK, P], F32).ap()
        queue_out = nc.dram_tensor("queue_out", [NE * CAP, P], F32).ap()

        cst = sb("cst", [P, NCONST])
        ident = cst[:, C_ID:C_ID + P]
        cos_qk, sin_qk = cst[:, C_COS:C_COS + 2 * P], cst[:, C_SIN:C_SIN + 2 * P]
        iota2 = cst[:, C_IOTA:C_IOTA + 2 * NE].rearrange("p (k e) -> p k e", k=2)
        ident_bf = sb("ident_bf", [P, P], BF16)
        causal_bf = sb("causal_bf", [P, P], BF16)
        tri_bf = sb("tri_bf", [P, P], BF16)
        ones_bf = sb("ones_bf", [P, P], BF16)
        mask_i32 = sb("mask_i32", [P, NB * P], I32)
        mask_neg = sb("mask_neg", [P, NB * P], BF16)
        mask_all = sb("mask_all", [P, NB * P], BF16)
        x_all = sb("x_all", [P, NB, P])
        x1_all = sb("x1_all", [P, NB, P])
        z_all = sb("z_all", [P, NB, P])
        wq_sb, wk_sb, wv_sb = sb("wq_sb", [P, INNER]), sb("wk_sb", [P, INNER]), sb("wv_sb", [P, INNER])
        wo_sb = sb("wo_sb", [P, INNER // P, P])
        bo_bc = sb("bo_bc", [P, P])
        wqkv_sb = sb("wqkv_sb", [P, 3 * P])
        w4_sb = sb("w4_sb", [P, 4, P])
        wvs_sb = sb("wvs_sb", [P, P])
        wproj_sb = sb("wproj_sb", [P, P])
        wgate_sb = sb("wgate_sb", [P, NE])
        gates2 = sb("gates2", [P, 2])
        tanh2 = sb("tanh2", [P, 2])
        NV = 4 + NE * MT
        rows = sb("rows", [NV, P])
        cols = sb("cols", [P, NV])
        zero = sb("zero", [P, 512])
        stats_x = sb("stats_x", [P, NB, 6])
        mv_x = sb("mv_x", [P, NB, 2])
        ve_x = sb("ve_x", [P, NB])
        rstd_x = sb("rstd_x", [P, NB])

        tiny = sb("tiny", [P, 3])

        xn = sb("xn", [P, P])
        c_sb = sb("c_sb", [P, P])
        xcT = sb("xcT", [P, 2 * P])
        qT = sb("qT", [P, INNER // P, P])
        kz = sb("kz", [P, INNER // P, 2, P])
        v_sb = sb("v_sb", [P, INNER])
        nmax_a, nmax_b = sb("nmax_a", [P, XH]), sb("nmax_b", [P, SH])
        sum_a, sum_b = sb("sum_a", [P, XH]), sb("sum_b", [P, SH])
        rec_a, rec_b = sb("rec_a", [P, XH]), sb("rec_b", [P, SH])
        p_a, p_b = sb("p_a", [P, 2, HC, P]), sb("p_b", [P, 2, HC, P])
        pT_a, pT_b = sb("pT_a", [P, HC, P]), sb("pT_b", [P, HC, P])
        oT_a = sb("oT_a", [P, 4, P])
        st_a, mv_a, ve_a, rs_a = sb("st_a", [P, 2, 6]), sb("mv_a", [P, 2, 2]), sb("ve_a", [P, 2]), sb("rs_a", [P, 2])

        h_sb = sb("h_sb", [P, P])
        hT = sb("hT", [P, P])
        rope1, rope2 = sb("rope1", [P, 2 * P]), sb("rope2", [P, 2 * P])
        kr = sb("kr", [P, P])
        qz = sb("qz", [P, 4, P])
        km = sb("km", [P, HC, P])
        v_pad = sb("v_pad", [P, SH, HC * SD])
        oT_b = sb("oT_b", [P, P])
        st_b, mv_b, ve_b, rs_b = sb("st_b", [P, 6]), sb("mv_b", [P, 2]), sb("ve_b", [P, 1]), sb("rs_b", [P, 1])

        h2n = sb("h2n", [P, P])
        h2s = sb("h2s", [P, P])
        h2T = sb("h2T", [P, P])
        r_nmax, r_exp, r_sum, r_rec = sb("r_nmax", [P, 1]), sb("r_exp", [P, NE]), sb("r_sum", [P, 1]), sb("r_rec", [P, 1])
        r_gate, r_top, r_idx, r_idxf = sb("r_gate", [P, NE]), sb("r_top", [P, 8]), sb("r_idx", [P, 8], U32), sb("r_idxf", [P, TOPK])
        r_mk = sb("r_mk", [P, TOPK, NE])
        r_mask = sb("r_mask", [P, NE], BF16)
        r_acc = sb("r_acc", [P, NE], BF16)
        r_pm = sb("r_pm", [P, TOPK, NE])
        r_pos = sb("r_pos", [P, TOPK])
        r_keep, r_kept, r_drop, r_row, r_pmin = (sb(n, [P, TOPK]) for n in ("r_keep", "r_kept", "r_drop", "r_row", "r_pmin"))
        r_slot = sb("r_slot", [P, TOPK], U32)
        gate_all = sb("gate_all", [P, NB, TOPK])
        from_all = sb("from_all", [P, NB, TOPK], U32)

        w1_sb = sb("w1_sb", [P, RING, FF])
        w2_sb = sb("w2_sb", [P, RING, MT, P])
        b2_bc = sb("b2_bc", [P, NE, P])
        xin = sb("xin", [P, RING, 2, P])
        xT = sb("xT", [P, 2, 2 * P])
        hid = sb("hid", [P, 2, MT, 2 * P])
        eo = sb("eo", [P, 2, 2, P])
        got = sb("got", [P, NB, TOPK, P])
        acc = sb("acc", [P, 2, P])
        res = sb("res", [P, NB, P])

        bk = [bank(f"bank{n}") for n in range(8)]
        s_a, s_b, t_a, t_b, o_a, o_b, y_bank, c_bank = bk
        q_banks, k_banks, v_banks = (s_a, o_a), (t_a, y_bank), (o_a, t_b)

        d_x, d_cst, d_rows, d_small, d_mask = sem("d_x"), sem("d_cst"), sem("d_rows"), sem("d_small"), sem("d_mask")
        d_wq, d_wk, d_wv, d_wo, d_wqkv = sem("d_wq"), sem("d_wk"), sem("d_wv"), sem("d_wo"), sem("d_wqkv")
        d_x0, d_proj = sem("d_x0"), sem("d_proj")
        d_zero, d_b2 = sem("d_zero"), sem("d_b2")
        d_ctx = signal("d_ctx", 16)
        zeroed, prep_pool = sem("zeroed"), sem("prep_pool")
        prep = sem("prep")
        consts_ready, vars_ready, rstd_ready = sem("consts_ready"), sem("vars_ready"), sem("rstd_ready")
        rows_turned, cols_ready, tanh_ready = sem("rows_turned"), sem("cols_ready"), sem("tanh_ready")
        bo_scaled = sem("bo_scaled")
        xb_ready, w4_ready = sem("xb_ready"), sem("w4_ready")
        xn_ready = signal("xn_ready", 1)
        xc_turned = signal("xc_turned", 1)
        xcT_ready = signal("xcT_ready", 1)
        q_made, k_made, v_made = signal("q_made", 2), signal("k_made", 2), signal("v_made", 2)
        q_ready, k_ready0, k_ready1 = signal("q_ready", 2), signal("k_ready0", 2), signal("k_ready1", 2)
        v_ready0, v_ready1 = signal("v_ready0", 1), signal("v_ready1", 1)
        a_scores, a_max, a_exp, a_rec, a_norm = (signal(n, CHUNKS) for n in ("a_scores", "a_max", "a_exp", "a_rec", "a_norm"))
        a_turned, a_pT, a_pv = (signal(n, CHUNKS) for n in ("a_turned", "a_pT", "a_pv"))
        a_oT = signal("a_oT", 2)
        a_y = signal("a_y", 1)
        a_x1 = signal("a_x1", 1)
        a_chain = signal("a_chain", 5)
        a_var = signal("a_var", 2)
        a_rstd = signal("a_rstd", 2)
        h_ready = signal("h_ready", 1)
        h_turned, hT_ready = signal("h_turned", 1), signal("hT_ready", 1)
        qk_made, qk_read, qkm_ready = signal("qk_made", 1), signal("qk_read", 1), signal("qkm_ready", 1)
        vs_made, vs_ready = signal("vs_made", 1), signal("vs_ready", 1)
        b_scores, b_max, b_exp, b_rec, b_norm = (signal(n, CHUNKS) for n in ("b_scores", "b_max", "b_exp", "b_rec", "b_norm"))
        b_turned, b_pT = signal("b_turned", CHUNKS), signal("b_pT", CHUNKS)
        b_pv, b_oT, b_proj = signal("b_pv", 1), signal("b_oT", 1), signal("b_proj", 1)
        rope_ready, b_x2 = signal("rope_ready", 1), signal("b_x2", 1)
        b_chain, b_var, b_rstd, h2n_ready = signal("b_chain", 2), signal("b_var", 1), signal("b_rstd", 1), signal("h2n_ready", 1)
        h2_turned, h2T_ready = signal("h2_turned", 1), signal("h2T_ready", 1)
        logits_made, lmax_ready, lexp_ready = signal("logits_made", 1), signal("lmax_ready", 1), signal("lexp_ready", 1)
        choice_ready, pos_made, pos_read = signal("choice_ready", 1), signal("pos_made", 1), signal("pos_read", 1)
        c_chain, slots_ready = signal("c_chain", 12), signal("slots_ready", 1)
        h2s_ready = signal("h2s_ready", 1)
        d_scatter = signal("d_scatter", 32)
        d_w = [signal(f"d_w{n}", 32) for n in range(RING)]
        d_xin = [signal(f"d_xin{n}", 16) for n in range(RING)]
        d_eo = [signal(f"d_eo{n}", 16) for n in range(2)]
        x_turned, xT_ready, h_made, h_act = signal("x_turned", 1), signal("xT_ready", 1), signal("h_made", 2), signal("h_act", MT)
        e_made, eo_ready = signal("e_made", 1), signal("eo_ready", 1)
        d_got, d_out = [signal(f"d_got{n}", 32) for n in range(NB)], sem("d_out")
        mix_chain, mixed = signal("mix_chain", 2), signal("mixed", 1)

        def batches(eng, body):
            def step(i):
                body(*((i - n if not isinstance(i, int) or 0 <= i - n < NB else None) for n in range(3)))
            first, last = (3, NB - 1) if LOOP else (NB + 2, NB + 2)
            for i in range(first):
                step(i)
            if LOOP:
                with eng.Fori(first, last) as i:
                    step(i)
            for i in range(last, NB + 2):
                step(i)

        def has_next(a):
            return not isinstance(a, int) or a + 1 < NB

        def later(batch):
            return not isinstance(batch, int) or batch > 0

        block = stack.enter_context(nc.Block())

        @block.sync
        def _(sp):
            sp.dma_start(x_all[:, 0, :], x[0]).then_inc(d_x0, 16)
            sp.dma_start(c_sb[:], ctx_in[0]).then_inc(d_ctx.sem, 16)
            sp.dma_start(wq_sb[:], wq).then_inc(d_wq, 16)
            sp.dma_start(x_all[:, 1:NB, :], x[1:NB].rearrange("b t d -> t b d")).then_inc(d_x, 16)
            sp.dma_start(wk_sb[:], wk).then_inc(d_wk, 16)
            sp.dma_start(mask_i32[:], mask.rearrange("(o b) t -> o (b t)", o=1).partition_broadcast(P)).then_inc(d_mask, 16)
            sp.dma_start(gates2[:, 0:1], g_x.partition_broadcast(P)).then_inc(d_small, 16)
            sp.dma_start(gates2[:, 1:2], g_f.partition_broadcast(P)).then_inc(d_small, 16)
            sp.dma_start(bo_bc[:], bo.partition_broadcast(P)).then_inc(d_small, 16)
            sp.dma_start(wqkv_sb[:], wqkv).then_inc(d_wqkv, 16)
            sp.dma_start(wv_sb[:], wv).then_inc(d_wv, 16)
            for n, v in enumerate((ln1_g, ln1_b, ln2_g, ln2_b)):
                sp.dma_start(rows[n:n + 1, :], v.rearrange("(o d) -> o d", o=1)).then_inc(d_rows, 16)
            sp.dma_start(rows[4:NV, :], b1.rearrange("e (m p) -> (e m) p", p=P)).then_inc(d_rows, 16)
            sp.dma_start(wo_sb[:], wo.rearrange("(t p) d -> p t d", p=P)).then_inc(d_wo, 16)
            sp.dma_start(wproj_sb[:], wproj).then_inc(d_proj, 16)
            sp.dma_start(wgate_sb[:], wgate).then_inc(d_proj, 16)
            sp.wait_ge(zeroed, 1)
            for n in range(NE * CAP * P // (P * 512)):
                sp.dma_start(queue_in[n * 512:(n + 1) * 512, :].rearrange("(p r) d -> p (r d)", p=P),
                             zero[:]).then_inc(d_zero, 16)
            sp.dma_start(b2_bc[:].rearrange("p e d -> p (e d)"),
                         b2.rearrange("(o e) d -> o (e d)", o=1).partition_broadcast(P)).then_inc(d_b2, 16)

            def weights(e, j):
                sp.dma_start(w1_sb[:, j, :], w1[e]).then_inc(d_w[j].sem, 16)
                sp.dma_start(w2_sb[:, j, :, :], w2[e].rearrange("(m p) d -> p m d", p=P)).then_inc(d_w[j].sem, 16)

            def body(a, b, c):
                if a is not None and has_next(a):
                    xc_turned.wait(sp, a)
                    sp.dma_start(c_sb[:], ctx_in[a + 1]).then_inc(d_ctx.sem, 16)
            batches(sp, body)
            for e in range(RING):
                weights(e, e)
            d_scatter.wait(sp, NB - 1)
            for e in range(NE):
                if e >= RING:
                    e_made.wait(sp, e - RING)
                    weights(e, e % RING)
                sp.dma_start(xin[:, e % RING, :, :],
                             queue_in[e * CAP:(e + 1) * CAP, :].rearrange("(t p) d -> p t d", p=P)).then_inc(d_xin[e % RING].sem, 16)
            for n in range(NB):
                mixed.wait(sp, n)
                sp.dma_start(out[n], res[:, n, :]).then_inc(d_out, 16)
            sp.wait_ge(d_out, 16 * NB)

        @block.gpsimd
        def _(pool):
            for blank in (kz, qz, v_pad):
                nc.gpsimd.memset(blank[:], 0.0).then_inc(prep_pool, 1)
            nc.gpsimd.memset(ones_bf[:], 1.0).then_inc(prep_pool, 1)
            nc.gpsimd.memset(r_acc[:], 0.0).then_inc(prep_pool, 1)
            pool.wait_ge(d_cst, 16)
            pool.wait_ge(vars_ready, 1)
            nc.gpsimd.tensor_tensor(rstd_x[:, 0:1], ve_x[:, 0:1], cst[:, C_POW:C_POW + 1], ALU.pow).then_inc(rstd_ready, 1)
            nc.gpsimd.memset(zero[:], 0.0).then_inc(zeroed, 1)
            pool.wait_ge(vars_ready, 2)
            nc.gpsimd.tensor_tensor(rstd_x[:, 1:NB], ve_x[:, 1:NB], cst[:, C_POW + 1:C_POW + NB], ALU.pow).then_inc(rstd_ready, 1)
            pool.wait_ge(tanh_ready, 1)
            nc.gpsimd.tensor_tensor(bo_bc[:], bo_bc[:], tanh2[:, 0:1].broadcast_to([P, P]), ALU.mult).then_inc(bo_scaled, 1)
            pool.wait_ge(bo_scaled, 1)
            nc.gpsimd.tensor_tensor(x1_all[:], x_all[:], bo_bc[:].unsqueeze(1).broadcast_to([P, NB, P]),
                                    ALU.add).then_inc(xb_ready, 1)

            def spare_pool(n):
                nc.gpsimd.tensor_tensor(tiny[:, n:n + 1], cst[:, C_POW:C_POW + 1], cst[:, C_POW:C_POW + 1], ALU.mult)

            def norm(batch, k, rec, p_buf, rec_s, norm_s):
                rec_s.wait(pool, batch, k + 1)
                nc.gpsimd.tensor_tensor(p_buf[:, k % 2], p_buf[:, k % 2],
                                        rec[:, HC * k:HC * k + HC].unsqueeze(2).broadcast_to([P, HC, P]),
                                        ALU.mult).then_inc(norm_s.sem, 1)

            def rstd(batch, n, var_s, ve, rs, rstd_s):
                var_s.wait(pool, batch, n + 1)
                nc.gpsimd.tensor_tensor(rs[:, n:n + 1], ve[:, n:n + 1], cst[:, C_POW:C_POW + 1],
                                        ALU.pow).then_inc(rstd_s.sem, 1)

            def norm_a(a, k):
                norm(a, k, rec_a, p_a, a_rec, a_norm)

            def norm_b(b, k):
                norm(b, k, rec_b, p_b, b_rec, b_norm)

            def rstd_a(b, n):
                rstd(b, n, a_var, ve_a, rs_a, a_rstd)

            def rstd_b(c):
                rstd(c, 0, b_var, ve_b, rs_b, b_rstd)

            def keep_rows(c):
                if later(c):
                    d_scatter.wait(pool, c - 1)
                h2n_ready.wait(pool, c, carrier=lambda: spare_pool(1))
                nc.gpsimd.tensor_copy(h2s[:], h2n[:]).then_inc(h2s_ready.sem, 1)

            def scatter(c):
                if isinstance(c, int) and c == 0:
                    pool.wait_ge(d_zero, 16 * NE * CAP // 512)
                slots_ready.wait(pool, c)
                h2s_ready.wait(pool, c, carrier=lambda: spare_pool(2))
                for k in range(TOPK):
                    pool.indirect_dma_start(out=queue_in, out_offset=bass.IndirectOffsetOnAxis(ap=r_slot[:, k:k + 1], axis=0),
                                            in_=h2s[:], in_offset=None).then_inc(d_scatter.sem, 16)

            def body(a, b, c):
                if b is not None:
                    rstd_a(b, 0)
                    rstd_a(b, 1)
                if c is not None:
                    norm_b(c, 3)
                    rstd_b(c)
                if a is not None:
                    norm_a(a, 0)
                if c is not None:
                    keep_rows(c)
                if a is not None:
                    norm_a(a, 1)
                if b is not None:
                    norm_b(b, 0)
                if a is not None:
                    norm_a(a, 2)
                if b is not None:
                    norm_b(b, 1)
                if a is not None:
                    norm_a(a, 3)
                if b is not None:
                    norm_b(b, 2)
                if c is not None:
                    scatter(c)
            batches(pool, body)
            for half in range(2):
                d_eo[half].wait(pool, NE // 2 - 1)
            for n in range(NB):
                for k in range(TOPK):
                    pool.indirect_dma_start(out=got[:, n, k, :], out_offset=None, in_=queue_out,
                                            in_offset=bass.IndirectOffsetOnAxis(ap=from_all[:, n, k:k + 1], axis=0)
                                            ).then_inc(d_got[n].sem, 16)

        @block.scalar
        def _(act):
            act.dma_start(cst[:], const).then_inc(d_cst, 16)

            def turn_xc(a):
                xc_turned.wait(act, a)
                nc.scalar.copy(xcT[:], o_b[:, 0:2 * P]).then_inc(xcT_ready.sem, 1)

            def exps(batch, k, bank_, nmax, sums, p_buf, max_s, turned_s, exp_s):
                max_s.wait(act, batch, k + 1)
                if k >= 2:
                    turned_s.wait(act, batch, k - 1)
                elif later(batch):
                    turned_s.wait(act, batch - 1, CHUNKS + k - 1)
                for j in range(HC):
                    n = HC * k + j
                    last = nc.scalar.activation(p_buf[:, k % 2, j, :], bank_[:, j * P:(j + 1) * P], ACT.Exp,
                                                bias=nmax[:, n:n + 1], accum_out=sums[:, n:n + 1])
                last.then_inc(exp_s.sem, 1)

            turn_xc(0)
            act.wait_ge(d_small, 48)
            nc.scalar.activation(tanh2[:], gates2[:], ACT.Tanh).then_inc(tanh_ready, 1)

            def exps_a(a, k):
                exps(a, k, s_a, nmax_a, sum_a, p_a, a_max, a_turned, a_exp)

            def exps_b(b, k):
                exps(b, k, s_b, nmax_b, sum_b, p_b, b_max, b_turned, b_exp)

            def copy_pT_b(b, k):
                b_turned.wait(act, b, k + 1)
                nc.scalar.copy(pT_b[:].rearrange("p h t -> p (h t)"), t_b[:]).then_inc(b_pT.sem, 1)

            def copy_q(a, f):
                q_made.wait(act, a, f + 1)
                nc.scalar.mul(qT[:, 4 * f:4 * f + 4, :].rearrange("p m t -> p (m t)"), q_banks[f][:],
                              float(XD) ** -0.5).then_inc(q_ready.sem, 1)

            def copy_v(a):
                v_made.wait(act, a, 1)
                nc.scalar.copy(v_sb[:, 0:512], v_banks[0][:]).then_inc(v_ready0.sem, 1)

            def exp_logits(c):
                lmax_ready.wait(act, c)
                nc.scalar.activation(r_exp[:], c_bank[:, P:P + NE], ACT.Exp, bias=r_nmax[:],
                                     accum_out=r_sum[:]).then_inc(lexp_ready.sem, 1)

            def turn_next(a):
                if has_next(a):
                    turn_xc(a + 1)

            def copy_k(a, f):
                k_made.wait(act, a, f + 1)
                nc.scalar.copy(kz[XD:P, 4 * f:4 * f + 4, 1, :],
                               k_banks[f][XD:P, :].rearrange("p (m t) -> p m t", m=4)).then_inc(k_ready1.sem, 1)

            def body(a, b, c):
                if a is not None:
                    copy_q(a, 0)
                    copy_q(a, 1)
                if c is not None:
                    copy_pT_b(c, 2)
                if a is not None:
                    copy_k(a, 0)
                    copy_k(a, 1)
                if c is not None:
                    copy_pT_b(c, 3)
                if a is not None:
                    exps_a(a, 0)
                    copy_v(a)
                    exps_a(a, 1)
                if b is not None:
                    exps_b(b, 0)
                if a is not None:
                    exps_a(a, 2)
                if b is not None:
                    exps_b(b, 1)
                if c is not None:
                    exp_logits(c)
                if a is not None:
                    exps_a(a, 3)
                    turn_next(a)
                if b is not None:
                    copy_pT_b(b, 0)
                    exps_b(b, 2)
                    copy_pT_b(b, 1)
                    exps_b(b, 3)
            batches(act, body)
            for e in range(NE):
                for m in range(MT):
                    h_made.wait(act, e, m // 2 + 1)
                    if m == 0 and e >= 2:
                        e_made.wait(act, e - 2)
                    hb = bk[1 + 2 * (e % 2) + m // 2]
                    nc.scalar.activation(hid[:, e % 2, m, :], hb[:, (m % 2) * 256:(m % 2) * 256 + 256], ACT.Gelu,
                                         bias=cols[:, 4 + e * MT + m:5 + e * MT + m]).then_inc(h_act.sem, 1)
                eo_ready.wait(act, e)
                act.dma_start(queue_out[e * CAP:(e + 1) * CAP, :].rearrange("(t p) d -> p t d", p=P),
                              eo[:, e % 2, :, :]).then_inc(d_eo[e % 2].sem, 16)

        @block.vector
        def _(dve):
            n_prep = [0]

            def link(ins):
                n_prep[0] += 1
                ins.then_inc(prep, 1)
                dve.wait_ge(prep, n_prep[0])

            def variances(first, last):
                for n in range(first, last):
                    ins = nc.vector.bn_stats(stats_x[:, n, :], x_all[:, n, :])
                link(ins)
                for n in range(first, last):
                    ins = nc.vector.bn_aggr(mv_x[:, n, :], stats_x[:, n, :])
                link(ins)
                nc.vector.tensor_scalar(ve_x[:, first:last], mv_x[:, first:last, 1], EPS, None, ALU.add).then_inc(vars_ready, 1)

            def apply_xn(a):
                nc.vector.tensor_scalar(xn[:], x_all[:, a, :], mv_x[:, a, 0:1], rstd_x[:, bass.ds(a, 1)],
                                        ALU.subtract, ALU.mult).then_inc(xn_ready.sem, 1)

            dve.wait_ge(d_x0, 16)
            variances(0, 1)
            dve.wait_ge(d_cst, 16)
            nc.vector.tensor_copy(ident_bf[:], ident)
            nc.vector.tensor_copy(tri_bf[:], cst[:, C_TRI:C_TRI + P])
            link(nc.vector.tensor_copy(causal_bf[:], cst[:, C_CAUSAL:C_CAUSAL + P]))
            dve.wait_ge(rstd_ready, 1)
            apply_xn(0)
            dve.wait_ge(d_x, 16)
            variances(1, NB)
            dve.wait_ge(d_mask, 16)
            link(nc.vector.tensor_scalar(mask_neg[:], mask_i32[:], NEG, None, ALU.mult))
            nc.vector.tensor_tensor(mask_all[:].rearrange("p (b t) -> p b t", b=NB),
                                    mask_neg[:].rearrange("p (b t) -> p b t", b=NB),
                                    causal_bf[:].unsqueeze(1).broadcast_to([P, NB, P]), ALU.min).then_inc(consts_ready, 1)
            dve.wait_ge(prep_pool, 5)

            def weight_columns():
                dve.wait_ge(d_wqkv, 16)
                src = wqkv_sb[:].rearrange("p (h s d) -> p s h d", h=SH, s=3)
                for s in range(2):
                    dst = w4_sb[:, s, :].rearrange("p (h d) -> p h d", h=SH)
                    rot = w4_sb[:, 2 + s, :].rearrange("p (h d) -> p h d", h=SH)
                    nc.vector.tensor_copy(dst, src[:, s])
                    nc.vector.tensor_scalar(rot[:, :, 0:SD // 2], src[:, s, :, SD // 2:SD], -1.0, None, ALU.mult)
                    nc.vector.tensor_copy(rot[:, :, SD // 2:SD], src[:, s, :, 0:SD // 2])
                nc.vector.tensor_copy(wvs_sb[:].rearrange("p (h d) -> p h d", h=SH), src[:, 2]).then_inc(w4_ready, 1)

            def spare_dve():
                nc.vector.memset(tiny[:, 0:1], 0.0)

            a_links, b_links, c_links = Chain(dve, a_chain), Chain(dve, b_chain), Chain(dve, c_chain)

            def row_max(batch, k, bank_, nmax, scores_s, max_s):
                scores_s.wait(dve, batch, k + 1)
                nc.vector.tensor_reduce(nmax[:, HC * k:HC * k + HC], bank_[:].rearrange("p (h t) -> p h t", h=HC),
                                        AX.X, ALU.max, negate=True).then_inc(max_s.sem, 1)

            def recip(batch, k, sums, rec, exp_s, rec_s):
                exp_s.wait(dve, batch, k + 1)
                nc.vector.reciprocal(rec[:, HC * k:HC * k + HC], sums[:, HC * k:HC * k + HC]).then_inc(rec_s.sem, 1)

            def recip_a(a, k):
                recip(a, k, sum_a, rec_a, a_exp, a_rec)

            def recip_b(b, k):
                recip(b, k, sum_b, rec_b, b_exp, b_rec)

            def max_a(a, k):
                row_max(a, k, s_a, nmax_a, a_scores, a_max)

            def max_b(b, k):
                row_max(b, k, s_b, nmax_b, b_scores, b_max)

            def copy_pT_a(a, k):
                a_turned.wait(dve, a, k + 1)
                nc.vector.tensor_copy(pT_a[:].rearrange("p h t -> p (h t)"), t_a[:]).then_inc(a_pT.sem, 1)

            def copy_oT_a(a, half):
                a_pv.wait(dve, a, 2 * half + 2)
                nc.vector.tensor_copy(oT_a[:].rearrange("p m t -> p (m t)"), o_a[:]).then_inc(a_oT.sem, 1)

            def copy_k(a, f):
                k_made.wait(dve, a, f + 1)
                nc.vector.tensor_copy(kz[0:XD, 4 * f:4 * f + 4, 0, :],
                                      k_banks[f][0:XD, :].rearrange("p (m t) -> p m t", m=4)).then_inc(k_ready0.sem, 1)

            def x1_var(b):
                a_links.start(b)
                if isinstance(b, int) and b == 0:
                    dve.wait_ge(xb_ready, 1)
                a_y.wait(dve, b)
                nc.vector.scalar_tensor_tensor(out=x1_all[:, b, :], in0=y_bank[:, 0:P], scalar=tanh2[:, 0:1],
                                               in1=x1_all[:, b, :], op0=ALU.mult, op1=ALU.add).then_inc(a_x1.sem, 1)
                a_x1.wait(dve, b, carrier=spare_dve)
                a_links.link(nc.vector.bn_stats(st_a[:, 0, :], x1_all[:, b, :]), spare_dve)
                a_links.link(nc.vector.bn_aggr(mv_a[:, 0, :], st_a[:, 0, :]))
                nc.vector.tensor_scalar(ve_a[:, 0:1], mv_a[:, 0, 1:2], EPS, None, ALU.add).then_inc(a_var.sem, 1)

            def z_var(b):
                a_rstd.wait(dve, b, 1)
                a_links.link(nc.vector.tensor_scalar(z_all[:, b, :], x1_all[:, b, :], mv_a[:, 0, 0:1], rs_a[:, 0:1],
                                                     ALU.subtract, ALU.mult), spare_dve)
                a_links.link(nc.vector.bn_stats(st_a[:, 1, :], z_all[:, b, :]), spare_dve)
                a_links.link(nc.vector.bn_aggr(mv_a[:, 1, :], st_a[:, 1, :]))
                nc.vector.tensor_scalar(ve_a[:, 1:2], mv_a[:, 1, 1:2], EPS, None, ALU.add).then_inc(a_var.sem, 1)
                a_links.end()

            def norm_h(b):
                a_rstd.wait(dve, b, 2)
                nc.vector.tensor_scalar(h_sb[:], z_all[:, b, :], mv_a[:, 1, 0:1], rs_a[:, 1:2],
                                        ALU.subtract, ALU.mult).then_inc(h_ready.sem, 1)

            def copy_hT(b):
                if isinstance(b, int) and b == 0:
                    dve.wait_ge(rows_turned, 1)
                    nc.vector.tensor_copy(cols[:], c_bank[:, 3 * P:3 * P + NV]).then_inc(cols_ready, 1)
                    dve.wait_ge(cols_ready, 1)
                h_turned.wait(dve, b)
                nc.vector.tensor_scalar(hT[:], c_bank[:, 0:P], cols[:, 0:1], cols[:, 1:2],
                                        ALU.mult, ALU.add).then_inc(hT_ready.sem, 1)

            def copy_oT_b(c):
                b_pv.wait(dve, c)
                nc.vector.tensor_copy(oT_b[:], o_b[:, 0:P]).then_inc(b_oT.sem, 1)

            def x2_var(c):
                b_links.start(c)
                b_proj.wait(dve, c)
                nc.vector.tensor_tensor(z_all[:, c, :], o_b[:, 2 * P:3 * P], z_all[:, c, :], ALU.add).then_inc(b_x2.sem, 1)
                b_x2.wait(dve, c, carrier=spare_dve)
                b_links.link(nc.vector.bn_stats(st_b[:], z_all[:, c, :]), spare_dve)
                b_links.link(nc.vector.bn_aggr(mv_b[:], st_b[:]))
                b_links.end()
                nc.vector.tensor_scalar(ve_b[:], mv_b[:, 1:2], EPS, None, ALU.add).then_inc(b_var.sem, 1)

            def norm_h2(c):
                b_rstd.wait(dve, c)
                nc.vector.tensor_scalar(h2n[:], z_all[:, c, :], mv_b[:, 0:1], rs_b[:, 0:1],
                                        ALU.subtract, ALU.mult).then_inc(h2n_ready.sem, 1)

            def copy_v(a):
                v_made.wait(dve, a, 2)
                nc.vector.tensor_copy(v_sb[:, 512:1024], v_banks[1][:]).then_inc(v_ready1.sem, 1)

            def next_xn(a):
                if isinstance(a, int) and a == 0:
                    weight_columns()
                    dve.wait_ge(rstd_ready, 2)
                if has_next(a):
                    apply_xn(a + 1)

            def rope(b):
                qk_made.wait(dve, b)
                nc.vector.tensor_tensor(rope1[:], y_bank[:, 0:2 * P], cos_qk, ALU.mult)
                nc.vector.tensor_tensor(rope2[:], y_bank[:, 2 * P:4 * P], sin_qk, ALU.mult).then_inc(qk_read.sem, 1)
                qk_read.wait(dve, b)
                nc.vector.tensor_tensor(kr[:], rope1[:, P:2 * P], rope2[:, P:2 * P], ALU.add).then_inc(rope_ready.sem, 1)
                for g in range(4):
                    r = slice(32 * g, 32 * g + 32)
                    nc.vector.tensor_tensor(qz[r, g, :], rope1[r, 0:P], rope2[r, 0:P], ALU.add)
                rope_ready.wait(dve, b)
                for j in range(HC):
                    last = nc.vector.tensor_scalar(km[:, j, :], kr[:], cst[:, C_HMASK + j:C_HMASK + j + 1], None, ALU.mult)
                last.then_inc(qkm_ready.sem, 1)

            def copy_vs(b):
                vs_made.wait(dve, b)
                nc.vector.tensor_copy(v_diag, c_bank[:, P:2 * P].rearrange("p (g j d) -> p g j d", g=4, j=HC)
                                      ).then_inc(vs_ready.sem, 1)

            def body(a, b, c):
                if c is not None:
                    recip_b(c, 2)
                if b is not None:
                    copy_oT_a(b, 1)
                if c is not None:
                    max_b(c, 3)
                if b is not None:
                    x1_var(b)
                    z_var(b)
                if c is not None:
                    recip_b(c, 3)
                if a is not None:
                    copy_k(a, 0)
                if b is not None:
                    norm_h(b)
                if a is not None:
                    copy_k(a, 1)
                if b is not None:
                    copy_hT(b)
                if c is not None:
                    copy_oT_b(c)
                if a is not None:
                    max_a(a, 0)
                if b is not None:
                    rope(b)
                if a is not None:
                    recip_a(a, 0)
                if c is not None:
                    x2_var(c)
                if a is not None:
                    max_a(a, 1)
                if b is not None:
                    max_b(b, 0)
                    copy_vs(b)
                if c is not None:
                    norm_h2(c)
                if a is not None:
                    recip_a(a, 1)
                    copy_pT_a(a, 0)
                    copy_v(a)
                    max_a(a, 2)
                if c is not None:
                    copy_h2T(c)
                if b is not None:
                    recip_b(b, 0)
                if a is not None:
                    copy_pT_a(a, 1)
                    next_xn(a)
                if b is not None:
                    max_b(b, 1)
                if a is not None:
                    recip_a(a, 2)
                    copy_oT_a(a, 0)
                if c is not None:
                    max_logits(c)
                if a is not None:
                    max_a(a, 3)
                    copy_pT_a(a, 2)
                if b is not None:
                    recip_b(b, 1)
                if c is not None:
                    choose(c)
                if a is not None:
                    recip_a(a, 3)
                if b is not None:
                    max_b(b, 2)
                if c is not None:
                    place(c)
                if a is not None:
                    copy_pT_a(a, 3)

            v_diag = v_pad[:].rearrange("p (g j) c -> p g (j c)", g=4)
            v_diag = bass.AP(tensor=v_diag.tensor, offset=v_diag.offset,
                             ap=[list(v_diag.ap[0]), [HC * HC * SD, 4], [HC * SD + SD, HC], [1, SD]])

            def copy_h2T(c):
                h2_turned.wait(dve, c)
                nc.vector.tensor_scalar(h2T[:], c_bank[:, 0:P], cols[:, 2:3], cols[:, 3:4],
                                        ALU.mult, ALU.add).then_inc(h2T_ready.sem, 1)

            def max_logits(c):
                logits_made.wait(dve, c)
                nc.vector.tensor_reduce(r_nmax[:], c_bank[:, P:P + NE], AX.X, ALU.max, negate=True).then_inc(lmax_ready.sem, 1)

            def choose(c):
                c_links.start(c)
                lexp_ready.wait(dve, c)
                c_links.link(nc.vector.reciprocal(r_rec[:], r_sum[:]))
                c_links.link(nc.vector.tensor_scalar(r_gate[:], r_exp[:], r_rec[:, 0:1], None, ALU.mult), spare_dve)
                c_links.link(nc.vector.max(r_top[:], r_gate[:]), spare_dve)
                c_links.link(nc.vector.max_index(r_idx[:], r_top[:], r_gate[:]))
                c_links.link(nc.vector.tensor_copy(r_idxf[:], r_idx[:, 0:TOPK]))
                c_links.link(nc.vector.tensor_tensor(r_mk[:], iota2, r_idxf[:].unsqueeze(2).broadcast_to([P, TOPK, NE]),
                                                     ALU.is_equal))
                nc.vector.tensor_tensor(r_mask[:], r_mk[:, 0, :], r_mk[:, 1, :], ALU.add).then_inc(choice_ready.sem, 1)

            def place(c):
                pos_made.wait(dve, c)
                nc.vector.tensor_tensor(r_pm[:], r_mk[:], c_bank[:, 256:256 + NE].unsqueeze(1).broadcast_to([P, TOPK, NE]),
                                        ALU.mult).then_inc(pos_read.sem, 1)
                pos_read.wait(dve, c)
                nc.vector.tensor_tensor(r_acc[:], r_acc[:], r_mask[:], ALU.add)
                c_links.link(nc.vector.tensor_reduce(r_pos[:], r_pm[:], AX.X, ALU.add))
                nc.vector.scalar_tensor_tensor(out=gate_all[:, c, :], in0=r_pos[:], scalar=float(CAP),
                                               in1=r_top[:, 0:TOPK], op0=ALU.is_le, op1=ALU.mult)
                nc.vector.tensor_scalar(r_keep[:], r_pos[:], float(CAP), None, ALU.is_le)
                nc.vector.scalar_tensor_tensor(out=r_drop[:], in0=r_pos[:], scalar=float(CAP),
                                               in1=cst_trash(c), op0=ALU.is_gt, op1=ALU.mult)
                c_links.link(nc.vector.tensor_scalar(r_pmin[:], r_pos[:], float(CAP), -1.0, ALU.min, ALU.add))
                c_links.link(nc.vector.scalar_tensor_tensor(out=r_row[:], in0=r_idxf[:], scalar=float(CAP), in1=r_pmin[:],
                                                            op0=ALU.mult, op1=ALU.add))
                c_links.link(nc.vector.tensor_copy(from_all[:, c, :], r_row[:]))
                c_links.link(nc.vector.tensor_tensor(r_kept[:], r_row[:], r_keep[:], ALU.mult))
                c_links.link(nc.vector.tensor_tensor(r_row[:], r_kept[:], r_drop[:], ALU.add))
                if later(c):
                    d_scatter.wait(dve, c - 1)
                nc.vector.tensor_copy(r_slot[:], r_row[:]).then_inc(slots_ready.sem, 1)
                c_links.end()

            trash = cst[:, C_TRASH:C_TRASH + 2 * NB].rearrange("p (b k) -> p b k", k=TOPK)

            def cst_trash(c):
                return trash[:, c, :]

            batches(dve, body)

            dve.wait_ge(d_b2, 16)

            def turned(e):
                x_turned.wait(dve, e)
                nc.vector.tensor_scalar(xT[:, e % 2, :], bk[0][:, 0:2 * P], cols[:, 2:3], cols[:, 3:4],
                                        ALU.mult, ALU.add).then_inc(xT_ready.sem, 1)
            turned(0)
            turned(1)
            for e in range(NE):
                if e + 2 < NE:
                    turned(e + 2)
                e_made.wait(dve, e)
                if e >= 2:
                    d_eo[e % 2].wait(dve, e // 2 - 1)
                nc.vector.tensor_tensor(eo[:, e % 2, :, :], bk[5 + e % 2][:, 0:2 * P].rearrange("p (t d) -> p t d", t=2),
                                        b2_bc[:, e, :].unsqueeze(1).broadcast_to([P, 2, P]), ALU.add).then_inc(eo_ready.sem, 1)
            mix = Chain(dve, mix_chain)
            for n in range(NB):
                d_got[n].wait(dve, 0)
                mix.start(n)
                mix.link(nc.vector.scalar_tensor_tensor(out=acc[:, 0, :], in0=got[:, n, 0, :], scalar=gate_all[:, n, 0:1],
                                                        in1=z_all[:, n, :], op0=ALU.mult, op1=ALU.add))
                mix.link(nc.vector.scalar_tensor_tensor(out=acc[:, 1, :], in0=got[:, n, 1, :], scalar=gate_all[:, n, 1:2],
                                                        in1=acc[:, 0, :], op0=ALU.mult, op1=ALU.add))
                nc.vector.scalar_tensor_tensor(out=res[:, n, :], in0=acc[:, 1, :], scalar=tanh2[:, 1:2],
                                               in1=x1_all[:, n, :], op0=ALU.mult, op1=ALU.add).then_inc(mixed.sem, 1)

        @block.tensor
        def _(pe):
            def turn_xc(a):
                xn_ready.wait(pe, a)
                d_ctx.wait(pe, a)
                nc.tensor.transpose(o_b[:, 0:P], xn[:], ident)
                nc.tensor.transpose(o_b[:, P:2 * P], c_sb[:], ident).then_inc(xc_turned.sem, 1)

            pe.wait_ge(d_cst, 16)
            turn_xc(0)

            def fill(a, w, half, banks, made, f):
                for m in range(4):
                    last = nc.tensor.matmul(banks[f][:, m * P:(m + 1) * P], w[:, (4 * f + m) * P:(4 * f + m + 1) * P],
                                            xcT[:, half * P:(half + 1) * P], start=True, stop=True)
                last.then_inc(made.sem, 1)

            def fill_q(a, f):
                if f == 0:
                    xcT_ready.wait(pe, a)
                    if isinstance(a, int) and a == 0:
                        pe.wait_ge(d_wq, 16)
                if later(a):
                    (a_exp, a_oT)[f].wait(pe, a - 1)
                fill(a, wq_sb, 0, q_banks, q_made, f)

            def fill_k(a, f):
                if isinstance(a, int) and a == 0:
                    pe.wait_ge(d_wk, 16)
                if later(a):
                    (a_pT, a_x1)[f].wait(pe, a - 1)
                fill(a, wk_sb, 1, k_banks, k_made, f)

            def fill_v(a, f):
                if isinstance(a, int) and a == 0:
                    pe.wait_ge(d_wv, 16)
                if f == 1 and (not isinstance(a, int) or a >= 2):
                    b_pT.wait(pe, a - 2)
                nc.tensor.matmul(v_banks[f][:], xcT[:, P:2 * P], wv_sb[:, f * 512:(f + 1) * 512],
                                 start=True, stop=True).then_inc(v_made.sem, 1)

            def turn_h(b):
                if isinstance(b, int) and b == 0:
                    pe.wait_ge(d_rows, 80)
                    nc.tensor.transpose(c_bank[:, 3 * P:3 * P + NV], rows[:], ident[0:NV, 0:NV]).then_inc(rows_turned, 1)
                    pe.wait_ge(cols_ready, 1)
                h_ready.wait(pe, b)
                if later(b):
                    if not isinstance(b, int) or b >= 2:
                        pos_read.wait(pe, b - 2)
                nc.tensor.transpose(c_bank[:, 0:P], h_sb[:], ident).then_inc(h_turned.sem, 1)

            def project_b(b):
                hT_ready.wait(pe, b)
                if isinstance(b, int) and b == 0:
                    pe.wait_ge(w4_ready, 1)
                if has_next(b):
                    k_ready0.wait(pe, b + 1)
                    k_ready1.wait(pe, b + 1)
                else:
                    a_x1.wait(pe, b)
                for n in range(4):
                    last = nc.tensor.matmul(y_bank[:, n * P:(n + 1) * P], w4_sb[:, n, :], hT[:], start=True, stop=True)
                last.then_inc(qk_made.sem, 1)
                nc.tensor.matmul(c_bank[:, P:2 * P], hT[:], wvs_sb[:], start=True, stop=True).then_inc(vs_made.sem, 1)

            def scores_a(a, k):
                if k == 0:
                    if isinstance(a, int) and a == 0:
                        pe.wait_ge(consts_ready, 1)
                    q_ready.wait(pe, a)
                    k_ready0.wait(pe, a)
                    k_ready1.wait(pe, a)
                else:
                    a_exp.wait(pe, a, k)
                nc.tensor.matmul(s_a[:], ident_bf[:], mask_all[:, bass.ts(a, P)].unsqueeze(1).broadcast_to([P, HC, P]),
                                 start=True, stop=False, skip_group_check=True)
                for n in range(2):
                    m = 2 * k + n
                    last = nc.tensor.matmul(s_a[:, n * 2 * P:(n + 1) * 2 * P], qT[:, m, :],
                                            kz[:, m, :, :].rearrange("p s t -> p (s t)"),
                                            start=False, stop=True, skip_group_check=True)
                last.then_inc(a_scores.sem, 1)

            def scores_b(b, k):
                if k == 0:
                    qkm_ready.wait(pe, b)
                else:
                    b_exp.wait(pe, b, k)
                nc.tensor.matmul(s_b[:], ident_bf[:], causal_bf[:].unsqueeze(1).broadcast_to([P, HC, P]),
                                 start=True, stop=False, skip_group_check=True)
                nc.tensor.matmul(s_b[:], qz[:, k, :], km[:].rearrange("p h t -> p (h t)"),
                                 start=False, stop=True, skip_group_check=True).then_inc(b_scores.sem, 1)

            def turn_p(batch, k, bank_, p_buf, norm_s, pT_s, turned_s):
                norm_s.wait(pe, batch, k + 1)
                if k >= 1:
                    pT_s.wait(pe, batch, k)
                for j in range(HC):
                    last = nc.tensor.transpose(bank_[:, j * P:(j + 1) * P], p_buf[:, k % 2, j, :], ident)
                last.then_inc(turned_s.sem, 1)

            def turn_a(a, k):
                turn_p(a, k, t_a, p_a, a_norm, a_pT, a_turned)

            def turn_b(b, k):
                if k == 0 and has_next(b):
                    v_ready1.wait(pe, b + 1)
                turn_p(b, k, t_b, p_b, b_norm, b_pT, b_turned)

            def pv_a(a, k):
                a_pT.wait(pe, a, k + 1)
                if k == 0:
                    v_ready0.wait(pe, a)
                if k == 2:
                    v_ready1.wait(pe, a)
                    a_oT.wait(pe, a, 1)
                for j in range(HC):
                    h = HC * k + j
                    r, m = XD * (h % 2), (h // 2) % 4
                    last = nc.tensor.matmul(o_a[r:r + XD, m * P:(m + 1) * P], v_sb[:, h * XD:(h + 1) * XD], pT_a[:, j, :],
                                            start=True, stop=True)
                last.then_inc(a_pv.sem, 1)

            def pv_b(b, g):
                b_pT.wait(pe, b, g + 1)
                if g == 0:
                    vs_ready.wait(pe, b)
                    if not isinstance(b, int) or b + 2 < NB:
                        xcT_ready.wait(pe, b + 2)
                for j in range(HC):
                    last = nc.tensor.matmul(o_b[32 * g:32 * g + 32, 0:P], v_pad[:, HC * g + j, :], pT_b[:, j, :],
                                            start=(j == 0), stop=(j == HC - 1))
                if g == CHUNKS - 1:
                    last.then_inc(b_pv.sem, 1)

            def output_a(a, half):
                a_oT.wait(pe, a, half + 1)
                if half == 0 and later(a):
                    qk_read.wait(pe, a - 1)
                if isinstance(a, int) and a == 0:
                    pe.wait_ge(d_wo, 16)
                for m in range(4):
                    last = nc.tensor.matmul(y_bank[:, 0:P], oT_a[:, m, :], wo_sb[:, 4 * half + m, :],
                                            start=(half == 0 and m == 0), stop=(half == 1 and m == 3))
                if half == 1:
                    last.then_inc(a_y.sem, 1)

            def output_b(c):
                if isinstance(c, int) and c == 0:
                    pe.wait_ge(d_proj, 32)
                b_oT.wait(pe, c)
                nc.tensor.matmul(o_b[:, 2 * P:3 * P], oT_b[:], wproj_sb[:], start=True, stop=True).then_inc(b_proj.sem, 1)

            def turn_h2(c):
                if has_next(c):
                    vs_ready.wait(pe, c + 1)
                h2n_ready.wait(pe, c)
                nc.tensor.transpose(c_bank[:, 0:P], h2n[:], ident).then_inc(h2_turned.sem, 1)

            def logits(c):
                h2T_ready.wait(pe, c)
                nc.tensor.matmul(c_bank[:, P:P + NE], h2T[:], wgate_sb[:], start=True, stop=True).then_inc(logits_made.sem, 1)

            def turn_next(a):
                if has_next(a):
                    if not isinstance(a, int) or a >= 2:
                        b_x2.wait(pe, a - 2)
                    turn_xc(a + 1)

            def positions(c):
                choice_ready.wait(pe, c)
                nc.tensor.matmul(c_bank[:, 256:256 + NE], tri_bf[:], r_mask[:], start=True, stop=False)
                nc.tensor.matmul(c_bank[:, 256:256 + NE], ones_bf[:], r_acc[:], start=False, stop=True).then_inc(pos_made.sem, 1)

            def body(a, b, c):
                if a is not None:
                    fill_q(a, 0)
                    fill_q(a, 1)
                if c is not None:
                    turn_b(c, 2)
                if a is not None:
                    fill_k(a, 0)
                if c is not None:
                    pv_b(c, 2)
                if a is not None:
                    fill_k(a, 1)
                if b is not None:
                    turn_h(b)
                if c is not None:
                    turn_b(c, 3)
                if b is not None:
                    project_b(b)
                if c is not None:
                    pv_b(c, 3)
                if a is not None:
                    scores_a(a, 0)
                    fill_v(a, 0)
                if c is not None:
                    output_b(c)
                if a is not None:
                    fill_v(a, 1)
                    scores_a(a, 1)
                if b is not None:
                    scores_b(b, 0)
                if a is not None:
                    turn_a(a, 0)
                if c is not None:
                    turn_h2(c)
                if a is not None:
                    scores_a(a, 2)
                    pv_a(a, 0)
                    turn_a(a, 1)
                if b is not None:
                    scores_b(b, 1)
                if a is not None:
                    pv_a(a, 1)
                    scores_a(a, 3)
                if c is not None:
                    logits(c)
                if a is not None:
                    turn_next(a)
                if b is not None:
                    turn_b(b, 0)
                if a is not None:
                    turn_a(a, 2)
                if b is not None:
                    scores_b(b, 2)
                if a is not None:
                    pv_a(a, 2)
                if b is not None:
                    pv_b(b, 0)
                if c is not None:
                    positions(c)
                if a is not None:
                    output_a(a, 0)
                if b is not None:
                    turn_b(b, 1)
                if a is not None:
                    turn_a(a, 3)
                if b is not None:
                    scores_b(b, 3)
                if a is not None:
                    pv_a(a, 3)
                if b is not None:
                    pv_b(b, 1)
                if a is not None:
                    output_a(a, 1)
            batches(pe, body)

            def turn_x(e):
                d_xin[e % RING].wait(pe, e // RING)
                if e >= 1:
                    xT_ready.wait(pe, e - 1)
                for t in range(2):
                    last = nc.tensor.transpose(bk[0][:, t * P:(t + 1) * P], xin[:, e % RING, t, :], ident)
                last.then_inc(x_turned.sem, 1)

            def hidden(e):
                xT_ready.wait(pe, e)
                d_w[e % RING].wait(pe, e // RING)
                if e >= 2:
                    h_act.wait(pe, e - 2)
                for m in range(MT):
                    last = nc.tensor.matmul(bk[1 + 2 * (e % 2) + m // 2][:, (m % 2) * 256:(m % 2) * 256 + 256],
                                            w1_sb[:, e % RING, m * P:(m + 1) * P], xT[:, e % 2, :], start=True, stop=True)
                    if m % 2:
                        last.then_inc(h_made.sem, 1)

            def expert_out(e):
                h_act.wait(pe, e)
                if e >= 2:
                    eo_ready.wait(pe, e - 2)
                for t in range(2):
                    for m in range(MT):
                        last = nc.tensor.matmul(bk[5 + e % 2][:, t * P:(t + 1) * P], hid[:, e % 2, m, t * P:(t + 1) * P],
                                                w2_sb[:, e % RING, m, :], start=(m == 0), stop=(m == MT - 1))
                last.then_inc(e_made.sem, 1)

            turn_x(0)
            for e in range(NE):
                hidden(e)
                if e + 1 < NE:
                    turn_x(e + 1)
                if e >= 1:
                    expert_out(e - 1)
            expert_out(NE - 1)


def constants():
    import numpy as np
    c = np.zeros((P, NCONST), np.float32)
    p, t = np.arange(P)[:, None], np.arange(P)[None, :]
    c[:, C_ID:C_ID + P] = p == t
    c[:, C_CAUSAL:C_CAUSAL + P] = np.where(t > p, np.float32(NEG), np.float32(0))
    c[:, C_TRI:C_TRI + P] = p <= t
    freq = (np.float32(1) / np.float32(10000) ** (np.arange(0, SD, 2, dtype=np.float32) / np.float32(SD))).astype(np.float32)
    angle = freq[np.arange(P) % (SD // 2)][:, None] * np.arange(P, dtype=np.float32)[None, :]
    for at, f in ((C_COS, np.cos), (C_SIN, np.sin)):
        c[:, at:at + P] = f(angle) * np.float32(SD ** -0.5)
        c[:, at + P:at + 2 * P] = f(angle)
    c[:, C_HMASK:C_HMASK + HC] = (p // SD) % HC == np.arange(HC)[None, :]
    c[:, C_IOTA:C_IOTA + 2 * NE] = np.tile(np.arange(NE), 2)[None, :]
    c[:, C_TRASH:C_TRASH + 2 * NB] = NE * CAP + np.arange(2 * NB)[None, :] * P + p
    c[:, C_POW:C_POW + NB] = -0.5
    return c


_INS = ['x', 'ctx_1024', 'mask_BxS2_bf0', 'g_xattn', 'g_ffn', 'L0_xattn_Wq', 'L0_xattn_Wk', 'L0_xattn_Wv', 'L0_xattn_Wo',
        'L0_xattn_bo', 'L0_ffn_ln1_g', 'L0_ffn_ln1_b', 'L0_ffn_Wqkv', 'L0_ffn_Wproj', 'L0_ffn_ln2_g', 'L0_ffn_ln2_b',
        'L0_ffn_Wgate', 'L0_ffn_W1', 'L0_ffn_b1', 'L0_ffn_W2', 'L0_ffn_b2']


def kernel(**inputs):
    import numpy as _np
    import concourse.bacc as _bacc
    from concourse import mybir as _mybir
    from concourse.bass_utils import run_bass_kernel_spmd as _run

    nc = _bacc.Bacc("TRN2", target_bir_lowering=False, num_devices=1)
    arrays, args = {}, []
    for name in _INS:
        a = _np.ascontiguousarray(inputs[name])
        if a.dtype.kind == "b":
            a = a.astype(_np.int32)
        arrays[f"in_{name}"] = a
    arrays["in_const"] = constants()
    for name, a in arrays.items():
        args.append(nc.dram_tensor(name, a.shape, _mybir.dt.from_np(a.dtype), kind="ExternalInput").ap())
    args.append(nc.dram_tensor("out_0", (NB, P, P), _mybir.dt.float32, kind="ExternalOutput").ap())
    build(nc, *args)
    r = _run(nc, [arrays], core_ids=[0])
    return r.results[0]["out_0"]
```

```python
from contextlib import ExitStack

import concourse.bass as bass
from concourse import mybir

F32 = mybir.dt.float32
BF16 = mybir.dt.bfloat16
U32 = mybir.dt.uint32
I32 = mybir.dt.int32
ALU = mybir.AluOpType
ACT = mybir.ActivationFunctionType
AX = mybir.AxisListType

P = 128
NB = 8
XH, XD = 16, 64
INNER = XH * XD
SH, SD = 16, 8
NE, FF = 8, 512
TOPK = 2
CAP = 2 * NB * P // NE
CHUNKS, HC = 4, 4
EPS = 1e-5
NEG = -(2.0 - 2.0 ** -7) * 2.0 ** 127
RING = 4
MT = FF // P
RW = P + 1
QR = NE * CAP // P

C_ID, C_CAUSAL, C_TRI = 0, P, 2 * P
C_COS = 3 * P
C_SIN = C_COS + 2 * P
C_HMASK = C_SIN + 2 * P
C_IOTA = C_HMASK + HC
C_TRASH = C_IOTA + 2 * NE
C_POW = C_TRASH + 2 * NB
C_FREE = C_POW + NB
NCONST = C_FREE + QR


class Signal:

    def __init__(self, sem, per):
        self.sem, self.per = sem, per

    def wait(self, eng, batch, k=None, carrier=None):
        eng.wait_ge(self.sem, batch * self.per + (self.per if k is None else k))
        if carrier is not None and not isinstance(batch, int):
            carrier()


class Chain:

    def __init__(self, eng, rises):
        self.eng, self.rises, self.n = eng, rises, 0

    def start(self, batch):
        self.batch, self.n = batch, 0

    def link(self, ins, carrier=None):
        self.n += 1
        ins.then_inc(self.rises.sem, 1)
        self.rises.wait(self.eng, self.batch, self.n, carrier)

    def end(self):
        assert self.n == self.rises.per, (self.n, self.rises.per)


def build(nc, x, ctx_in, mask, g_x, g_f, wq, wk, wv, wo, bo, ln1_g, ln1_b, wqkv, wproj, ln2_g, ln2_b,
          wgate, w1, b1, w2, b2, const, out):
    stack = ExitStack()
    with stack:
        def sb(name, shape, dt=F32):
            return stack.enter_context(nc.sbuf_tensor(name, shape, dt))

        def bank(name):
            return stack.enter_context(nc.psum_tensor(name, [P, 512], F32))

        def sem(name):
            return stack.enter_context(nc.semaphore(name))

        def signal(name, per):
            return Signal(sem(name), per)

        queue_in = nc.dram_tensor("queue_in", [NE * CAP + NB * P * TOPK, RW], F32).ap()
        results = nc.dram_tensor("results", [NB * TOPK * P + NE * CAP, P], F32).ap()

        cst = sb("cst", [P, NCONST])
        ident = cst[:, C_ID:C_ID + P]
        cos_qk, sin_qk = cst[:, C_COS:C_COS + 2 * P], cst[:, C_SIN:C_SIN + 2 * P]
        iota2 = cst[:, C_IOTA:C_IOTA + 2 * NE].rearrange("p (k e) -> p k e", k=2)
        ident_bf = sb("ident_bf", [P, P], BF16)
        causal_bf = sb("causal_bf", [P, P], BF16)
        tri_bf = sb("tri_bf", [P, P], BF16)
        ones_bf = sb("ones_bf", [P, P], BF16)
        mask_i32 = sb("mask_i32", [P, NB * P], I32)
        mask_neg = sb("mask_neg", [P, NB * P], BF16)
        mask_all = sb("mask_all", [P, NB * P], BF16)
        x_all = sb("x_all", [P, NB, P])
        x1_all = sb("x1_all", [P, NB, P])
        z_all = sb("z_all", [P, NB, P])
        wq_sb, wk_sb, wv_sb = sb("wq_sb", [P, INNER]), sb("wk_sb", [P, INNER]), sb("wv_sb", [P, INNER])
        wo_sb = sb("wo_sb", [P, INNER // P, P])
        bo_bc = sb("bo_bc", [P, P])
        wqkv_sb = sb("wqkv_sb", [P, 3 * P])
        w4_sb = sb("w4_sb", [P, 4, P])
        wvs_sb = sb("wvs_sb", [P, P])
        wproj_sb = sb("wproj_sb", [P, P])
        wgate_sb = sb("wgate_sb", [P, NE])
        gates2 = sb("gates2", [P, 2])
        tanh2 = sb("tanh2", [P, 2])
        NV = 4 + NE * MT
        rows = sb("rows", [NV, P])
        cols = sb("cols", [P, NV])
        blank = sb("blank", [P, QR, RW])
        stats_x = sb("stats_x", [P, NB, 6])
        mv_x = sb("mv_x", [P, NB, 2])
        ve_x = sb("ve_x", [P, NB])
        rstd_x = sb("rstd_x", [P, NB])

        tiny = sb("tiny", [P, 3])

        xn = sb("xn", [P, P])
        c_sb = sb("c_sb", [P, P])
        xcT = sb("xcT", [P, 2 * P])
        qT = sb("qT", [P, INNER // P, P])
        kz = sb("kz", [P, INNER // P, 2, P])
        v_sb = sb("v_sb", [P, INNER])
        nmax_a, nmax_b = sb("nmax_a", [P, XH]), sb("nmax_b", [P, SH])
        sum_a, sum_b = sb("sum_a", [P, XH]), sb("sum_b", [P, SH])
        rec_a, rec_b = sb("rec_a", [P, XH]), sb("rec_b", [P, SH])
        p_a, p_b = sb("p_a", [P, 2, HC, P]), sb("p_b", [P, 2, HC, P])
        pT_a, pT_b = sb("pT_a", [P, 2, HC, P]), sb("pT_b", [P, 2, HC, P])
        oT_a = sb("oT_a", [P, 4, P])
        st_a, mv_a, ve_a, rs_a = sb("st_a", [P, 2, 6]), sb("mv_a", [P, 2, 2]), sb("ve_a", [P, 2]), sb("rs_a", [P, 2])

        h_sb = sb("h_sb", [P, P])
        hT = sb("hT", [P, P])
        rope1, rope2 = sb("rope1", [P, 2 * P]), sb("rope2", [P, 2 * P])
        kr = sb("kr", [P, P])
        qz = sb("qz", [P, 4, P])
        km = sb("km", [P, HC, P])
        v_pad = sb("v_pad", [P, SH, HC * SD])
        oT_b = sb("oT_b", [P, P])
        st_b, mv_b, ve_b, rs_b = sb("st_b", [P, 6]), sb("mv_b", [P, 2]), sb("ve_b", [P, 1]), sb("rs_b", [P, 1])

        h2n = sb("h2n", [P, P])
        h2s = sb("h2s", [P, TOPK, RW])
        h2T = sb("h2T", [P, P])
        r_nmax, r_exp, r_sum, r_rec = sb("r_nmax", [P, 1]), sb("r_exp", [P, NE]), sb("r_sum", [P, 1]), sb("r_rec", [P, 1])
        r_gate, r_top, r_idx, r_idxf = sb("r_gate", [P, NE]), sb("r_top", [P, 8]), sb("r_idx", [P, 8], U32), sb("r_idxf", [P, TOPK])
        r_mk = sb("r_mk", [P, TOPK, NE])
        r_mask = sb("r_mask", [P, NE], BF16)
        r_acc = sb("r_acc", [P, NE], BF16)
        r_pm = sb("r_pm", [P, TOPK, NE])
        r_pos = sb("r_pos", [P, TOPK])
        r_keep, r_kept, r_drop, r_row, r_pmin = (sb(n, [P, TOPK]) for n in ("r_keep", "r_kept", "r_drop", "r_row", "r_pmin"))
        r_slot = sb("r_slot", [P, TOPK], U32)
        gate_all = sb("gate_all", [P, NB, TOPK])
        gate_t = sb("gate_t", [P, NB, TOPK])

        w1_sb = sb("w1_sb", [P, RING, FF])
        w2_sb = sb("w2_sb", [P, RING, MT, P])
        b2_bc = sb("b2_bc", [P, NE, P])
        xin = sb("xin", [P, RING, 2, RW])
        dest = sb("dest", [P, NE, 2], U32)
        xT = sb("xT", [P, 2, 2 * P])
        hid = sb("hid", [P, 2, MT, 2 * P])
        eo = sb("eo", [P, 2, 2, P])
        got = sb("got", [P, NB, TOPK, P])
        acc = sb("acc", [P, NB, P])
        res = sb("res", [P, NB, P])

        bk = [bank(f"bank{n}") for n in range(8)]
        s_a, s_b, t_a, t_b, o_a, o_b, y_bank, c_bank = bk
        q_banks, k_banks, v_banks = (s_a, o_a), (t_a, y_bank), (o_a, t_b)

        d_x, d_cst, d_rows, d_small, d_mask = sem("d_x"), sem("d_cst"), sem("d_rows"), sem("d_small"), sem("d_mask")
        d_wq, d_wk, d_wv, d_wo, d_wqkv = sem("d_wq"), sem("d_wk"), sem("d_wv"), sem("d_wo"), sem("d_wqkv")
        d_x0, d_proj = sem("d_x0"), sem("d_proj")
        d_zero, d_b2 = sem("d_zero"), sem("d_b2")
        d_ctx = signal("d_ctx", 16)
        zeroed, prep_pool = sem("zeroed"), sem("prep_pool")
        prep = sem("prep")
        consts_ready, vars_ready, rstd_ready = sem("consts_ready"), sem("vars_ready"), sem("rstd_ready")
        rows_turned, cols_ready, tanh_ready = sem("rows_turned"), sem("cols_ready"), sem("tanh_ready")
        bo_scaled = sem("bo_scaled")
        xb_ready, w4_ready = sem("xb_ready"), sem("w4_ready")
        xn_ready = signal("xn_ready", 1)
        xc_turned = signal("xc_turned", 1)
        xcT_ready = signal("xcT_ready", 1)
        q_made, k_made, v_made = signal("q_made", 2), signal("k_made", 2), signal("v_made", 2)
        q_ready, k_ready0, k_ready1 = signal("q_ready", 2), signal("k_ready0", 2), signal("k_ready1", 2)
        v_ready0, v_ready1 = signal("v_ready0", 1), signal("v_ready1", 1)
        a_scores, a_max, a_exp, a_rec, a_norm = (signal(n, CHUNKS) for n in ("a_scores", "a_max", "a_exp", "a_rec", "a_norm"))
        a_turned, a_pT, a_pv = (signal(n, CHUNKS) for n in ("a_turned", "a_pT", "a_pv"))
        a_oT = signal("a_oT", 2)
        a_y = signal("a_y", 1)
        a_x1 = signal("a_x1", 1)
        a_chain = signal("a_chain", 5)
        a_var = signal("a_var", 2)
        a_rstd = signal("a_rstd", 2)
        h_ready = signal("h_ready", 1)
        h_turned, hT_ready = signal("h_turned", 1), signal("hT_ready", 1)
        qk_made, qk_read, qkm_ready = signal("qk_made", 1), signal("qk_read", 1), signal("qkm_ready", 1)
        vs_made, vs_ready = signal("vs_made", 1), signal("vs_ready", 1)
        b_scores, b_max, b_exp, b_rec, b_norm = (signal(n, CHUNKS) for n in ("b_scores", "b_max", "b_exp", "b_rec", "b_norm"))
        b_turned, b_pT = signal("b_turned", CHUNKS), signal("b_pT", CHUNKS)
        b_pv, b_oT, b_proj = signal("b_pv", 1), signal("b_oT", 1), signal("b_proj", 1)
        rope_ready, qz_ready, b_x2 = signal("rope_ready", 1), signal("qz_ready", 1), signal("b_x2", 1)
        b_chain, b_var, b_rstd, h2n_ready = signal("b_chain", 2), signal("b_var", 1), signal("b_rstd", 1), signal("h2n_ready", 1)
        h2_turned, h2T_ready = signal("h2_turned", 1), signal("h2T_ready", 1)
        logits_made, lmax_ready, lexp_ready = signal("logits_made", 1), signal("lmax_ready", 1), signal("lexp_ready", 1)
        choice_ready, pos_made, pos_read = signal("choice_ready", 1), signal("pos_made", 1), signal("pos_read", 1)
        c_chain, slots_ready = signal("c_chain", 11), signal("slots_ready", 1)
        h2s_ready = signal("h2s_ready", 1)
        d_scatter = signal("d_scatter", 32)
        d_w = [signal(f"d_w{n}", 32) for n in range(RING)]
        d_xin = [signal(f"d_xin{n}", 16) for n in range(RING)]
        d_eo = [signal(f"d_eo{n}", 32) for n in range(2)]
        x_turned, xT_ready, h_made, h_act = signal("x_turned", 1), signal("xT_ready", 1), signal("h_made", 2), signal("h_act", MT)
        e_made, eo_ready = signal("e_made", 1), signal("eo_ready", 1)
        d_got, d_out = [signal(f"d_got{n}", 16) for n in range(NB)], sem("d_out")
        base_ready, half_mixed, mixed = sem("base_ready"), signal("half_mixed", 1), signal("mixed", 1)
        blank_zero = sem("blank_zero")

        def batches(eng, body, drain=None, fill_pipe=None):
            def step(i):
                abc = [i - n if not isinstance(i, int) or 0 <= i - n < NB else None for n in range(3)]
                if isinstance(i, int) and i == 0 and fill_pipe is not None:
                    fill_pipe(0)
                elif abc[0] is None and drain is not None:
                    drain(*abc[1:])
                else:
                    body(*abc)
            first, last = 3, NB - 1
            for i in range(first):
                step(i)
            with eng.Fori(0, (last - first) // 2) as n:
                step(n * 2 + first)
                step(n * 2 + first + 1)
            for i in range(last, NB + 2):
                step(i)

        def has_next(a):
            return not isinstance(a, int) or a + 1 < NB

        def sa_banks(a):
            return (s_a, s_a) if later(a) else (s_a, s_b)

        def ta_banks(a):
            return (t_a, t_a) if later(a) else (t_a, t_b)

        def s_banks(b):
            return (s_b, s_b) if has_next(b) else (s_b, s_a)

        def t_banks(b):
            return (t_b, t_b) if has_next(b) else (t_b, t_a)

        def later(batch):
            return not isinstance(batch, int) or batch > 0

        block = stack.enter_context(nc.Block())

        @block.sync
        def _(sp):
            sp.dma_start(x_all[:, 0, :], x[0]).then_inc(d_x0, 16)
            sp.dma_start(c_sb[:], ctx_in[0]).then_inc(d_ctx.sem, 16)
            sp.dma_start(wq_sb[:], wq).then_inc(d_wq, 16)
            sp.dma_start(x_all[:, 1:NB, :], x[1:NB].rearrange("b t d -> t b d")).then_inc(d_x, 16)
            sp.dma_start(wk_sb[:], wk).then_inc(d_wk, 16)
            sp.dma_start(mask_i32[:], mask.rearrange("(o b) t -> o (b t)", o=1).partition_broadcast(P)).then_inc(d_mask, 16)
            sp.dma_start(gates2[:, 0:1], g_x.partition_broadcast(P)).then_inc(d_small, 16)
            sp.dma_start(gates2[:, 1:2], g_f.partition_broadcast(P)).then_inc(d_small, 16)
            sp.dma_start(bo_bc[:], bo.partition_broadcast(P)).then_inc(d_small, 16)
            sp.dma_start(wqkv_sb[:], wqkv).then_inc(d_wqkv, 16)
            sp.dma_start(wv_sb[:], wv).then_inc(d_wv, 16)
            for n, v in enumerate((ln1_g, ln1_b, ln2_g, ln2_b)):
                sp.dma_start(rows[n:n + 1, :], v.rearrange("(o d) -> o d", o=1)).then_inc(d_rows, 16)
            sp.dma_start(rows[4:NV, :], b1.rearrange("e (m p) -> (e m) p", p=P)).then_inc(d_rows, 16)
            sp.dma_start(wo_sb[:], wo.rearrange("(t p) d -> p t d", p=P)).then_inc(d_wo, 16)
            sp.dma_start(wproj_sb[:], wproj).then_inc(d_proj, 16)
            sp.dma_start(wgate_sb[:], wgate).then_inc(d_proj, 16)

            def clear_queues():
                sp.wait_ge(zeroed, 1)
                sp.dma_start(queue_in[0:NE * CAP, :].rearrange("(p r) d -> p r d", p=P), blank[:]).then_inc(d_zero, 16)
                sp.dma_start(results[0:NE * CAP, :].rearrange("(p r) d -> p r d", p=P), blank[:, :, 0:P]).then_inc(d_zero, 16)
                sp.dma_start(b2_bc[:].rearrange("p e d -> p (e d)"),
                             b2.rearrange("(o e) d -> o (e d)", o=1).partition_broadcast(P)).then_inc(d_b2, 16)

            def weights(e, j):
                sp.dma_start(w1_sb[:, j, :], w1[e]).then_inc(d_w[j].sem, 16)
                sp.dma_start(w2_sb[:, j, :, :], w2[e].rearrange("(m p) d -> p m d", p=P)).then_inc(d_w[j].sem, 16)

            def body(a, b, c):
                if a is not None and has_next(a):
                    xc_turned.wait(sp, a)
                    sp.dma_start(c_sb[:], ctx_in[a + 1]).then_inc(d_ctx.sem, 16)
                if isinstance(a, int) and a == 0:
                    clear_queues()
            batches(sp, body)
            for e in range(RING):
                weights(e, e)
            d_scatter.wait(sp, NB - 1)
            for e in range(NE):
                if e >= RING:
                    e_made.wait(sp, e - RING)
                    weights(e, e % RING)
                sp.dma_start(xin[:, e % RING, :, :],
                             queue_in[e * CAP:(e + 1) * CAP, :].rearrange("(t p) d -> p t d", p=P)).then_inc(d_xin[e % RING].sem, 16)
            for half in range(2):
                d_eo[half].wait(sp, NE // 2 - 1)
            for n in range(0, NB, 2):
                sp.dma_start(got[:, n, :, :], results[n * TOPK * P:(n + 1) * TOPK * P, :].rearrange("(k p) d -> p k d", p=P)
                             ).then_inc(d_got[n].sem, 16)
            for n in range(1, NB, 2):
                mixed.wait(sp, n)
                sp.dma_start(out[n - 1:n + 1].rearrange("b t d -> t b d"), res[:, n - 1:n + 1, :]).then_inc(d_out, 16)
            sp.wait_ge(d_out, 16 * NB // 2)

        @block.gpsimd
        def _(pool):
            for padded in (kz, qz, v_pad):
                nc.gpsimd.memset(padded[:], 0.0).then_inc(prep_pool, 1)
            nc.gpsimd.memset(ones_bf[:], 1.0).then_inc(prep_pool, 1)
            nc.gpsimd.memset(r_acc[:], 0.0).then_inc(prep_pool, 1)
            pool.wait_ge(d_cst, 16)
            pool.wait_ge(vars_ready, 1)
            nc.gpsimd.tensor_tensor(rstd_x[:, 0:1], ve_x[:, 0:1], cst[:, C_POW:C_POW + 1], ALU.pow).then_inc(rstd_ready, 1)
            nc.gpsimd.memset(blank[:], 0.0).then_inc(blank_zero, 1)
            pool.wait_ge(vars_ready, 2)
            nc.gpsimd.tensor_tensor(rstd_x[:, 1:NB], ve_x[:, 1:NB], cst[:, C_POW + 1:C_POW + NB], ALU.pow).then_inc(rstd_ready, 1)
            pool.wait_ge(tanh_ready, 1)
            nc.gpsimd.tensor_tensor(bo_bc[:], bo_bc[:], tanh2[:, 0:1].broadcast_to([P, P]), ALU.mult).then_inc(bo_scaled, 1)
            pool.wait_ge(bo_scaled, 1)
            nc.gpsimd.tensor_tensor(x1_all[:], x_all[:], bo_bc[:].unsqueeze(1).broadcast_to([P, NB, P]),
                                    ALU.add).then_inc(xb_ready, 1)

            def spare_pool(n):
                nc.gpsimd.tensor_tensor(tiny[:, n:n + 1], cst[:, C_POW:C_POW + 1], cst[:, C_POW:C_POW + 1], ALU.mult)

            def norm(batch, k, rec, p_buf, rec_s, norm_s):
                rec_s.wait(pool, batch, k + 1)
                nc.gpsimd.tensor_tensor(p_buf[:, k % 2], p_buf[:, k % 2],
                                        rec[:, HC * k:HC * k + HC].unsqueeze(2).broadcast_to([P, HC, P]),
                                        ALU.mult).then_inc(norm_s.sem, 1)

            def rstd(batch, n, var_s, ve, rs, rstd_s):
                var_s.wait(pool, batch, n + 1)
                nc.gpsimd.tensor_tensor(rs[:, n:n + 1], ve[:, n:n + 1], cst[:, C_POW:C_POW + 1],
                                        ALU.pow).then_inc(rstd_s.sem, 1)

            def norm_a(a, k):
                norm(a, k, rec_a, p_a, a_rec, a_norm)

            def norm_b(b, k):
                norm(b, k, rec_b, p_b, b_rec, b_norm)

            def rstd_a(b, n):
                rstd(b, n, a_var, ve_a, rs_a, a_rstd)

            def rstd_b(c):
                rstd(c, 0, b_var, ve_b, rs_b, b_rstd)

            def keep_rows(c):
                if later(c):
                    d_scatter.wait(pool, c - 1)
                h2n_ready.wait(pool, c, carrier=lambda: spare_pool(1))
                nc.gpsimd.tensor_copy(h2s[:, :, 0:P], h2n[:].unsqueeze(1).broadcast_to([P, TOPK, P])).then_inc(h2s_ready.sem, 1)

            def scatter(c):
                if isinstance(c, int) and c == 0:
                    pool.wait_ge(d_zero, 32)
                slots_ready.wait(pool, c)
                h2s_ready.wait(pool, c, carrier=lambda: spare_pool(2))
                for k in range(TOPK):
                    pool.indirect_dma_start(out=queue_in, out_offset=bass.IndirectOffsetOnAxis(ap=r_slot[:, k:k + 1], axis=0),
                                            in_=h2s[:, k, :], in_offset=None).then_inc(d_scatter.sem, 16)

            def body(a, b, c):
                if c is not None:
                    norm_b(c, 3)
                if b is not None:
                    rstd_a(b, 0)
                    rstd_a(b, 1)
                if c is not None:
                    rstd_b(c)
                if a is not None:
                    norm_a(a, 0)
                    norm_a(a, 1)
                    norm_a(a, 2)
                if b is not None:
                    norm_b(b, 0)
                    norm_b(b, 1)
                if a is not None:
                    norm_a(a, 3)
                if c is not None:
                    keep_rows(c)
                if b is not None:
                    norm_b(b, 2)
                if c is not None:
                    scatter(c)

            def drain(b, c):
                if c is not None:
                    norm_b(c, 3)
                if b is not None:
                    rstd_a(b, 0)
                    rstd_a(b, 1)
                if c is not None:
                    rstd_b(c)
                if b is not None:
                    norm_b(b, 0)
                if c is not None:
                    keep_rows(c)
                if b is not None:
                    norm_b(b, 1)
                if c is not None:
                    scatter(c)
                if b is not None:
                    norm_b(b, 2)

            def fill_pipe(a):
                norm_a(a, 0)
                norm_a(a, 1)
                norm_a(a, 2)
                norm_a(a, 3)
            batches(pool, body, drain, fill_pipe)
            for e in range(NE):
                eo_ready.wait(pool, e)
                for t in range(2):
                    pool.indirect_dma_start(out=results, out_offset=bass.IndirectOffsetOnAxis(ap=dest[:, e, t:t + 1], axis=0),
                                            in_=eo[:, e % 2, t, :], in_offset=None).then_inc(d_eo[e % 2].sem, 16)

        @block.scalar
        def _(act):
            act.dma_start(cst[:], const).then_inc(d_cst, 16)

            def turn_xc(a):
                xc_turned.wait(act, a)
                nc.scalar.copy(xcT[:], o_b[:, 0:2 * P]).then_inc(xcT_ready.sem, 1)

            def exps(batch, k, bank_, nmax, sums, p_buf, max_s, turned_s, exp_s):
                max_s.wait(act, batch, k + 1)
                if k >= 2:
                    turned_s.wait(act, batch, k - 1)
                elif later(batch):
                    turned_s.wait(act, batch - 1, CHUNKS + k - 1)
                for j in range(HC):
                    n = HC * k + j
                    last = nc.scalar.activation(p_buf[:, k % 2, j, :], bank_[:, j * P:(j + 1) * P], ACT.Exp,
                                                bias=nmax[:, n:n + 1], accum_out=sums[:, n:n + 1])
                last.then_inc(exp_s.sem, 1)

            turn_xc(0)
            act.wait_ge(d_small, 48)
            nc.scalar.activation(tanh2[:], gates2[:], ACT.Tanh).then_inc(tanh_ready, 1)

            def exps_a(a, k):
                exps(a, k, sa_banks(a)[k % 2], nmax_a, sum_a, p_a, a_max, a_turned, a_exp)

            def exps_b(b, k):
                exps(b, k, s_banks(b)[k % 2], nmax_b, sum_b, p_b, b_max, b_turned, b_exp)

            def copy_pT_b(b, k):
                b_turned.wait(act, b, k + 1)
                nc.scalar.copy(pT_b[:, k % 2].rearrange("p h t -> p (h t)"), t_banks(b)[k % 2][:]).then_inc(b_pT.sem, 1)

            def copy_q(a, f):
                q_made.wait(act, a, f + 1)
                nc.scalar.mul(qT[:, 4 * f:4 * f + 4, :].rearrange("p m t -> p (m t)"), q_banks[f][:],
                              float(XD) ** -0.5).then_inc(q_ready.sem, 1)

            def copy_v(a):
                v_made.wait(act, a, 1)
                nc.scalar.copy(v_sb[:, 0:512], v_banks[0][:]).then_inc(v_ready0.sem, 1)

            def mask_k(b):
                rope_ready.wait(act, b)
                for j in range(HC):
                    last = nc.scalar.activation(km[:, j, :], kr[:], ACT.Copy, scale=cst[:, C_HMASK + j:C_HMASK + j + 1])
                last.then_inc(qkm_ready.sem, 1)

            def exp_logits(c):
                lmax_ready.wait(act, c)
                nc.scalar.activation(r_exp[:], c_bank[:, P:P + NE], ACT.Exp, bias=r_nmax[:],
                                     accum_out=r_sum[:]).then_inc(lexp_ready.sem, 1)

            def turn_next(a):
                if has_next(a):
                    turn_xc(a + 1)

            def copy_k(a, f):
                k_made.wait(act, a, f + 1)
                nc.scalar.copy(kz[XD:P, 4 * f:4 * f + 4, 1, :],
                               k_banks[f][XD:P, :].rearrange("p (m t) -> p m t", m=4)).then_inc(k_ready1.sem, 1)

            def body(a, b, c):
                if a is not None:
                    copy_k(a, 0)
                    copy_q(a, 0)
                    copy_k(a, 1)
                if c is not None:
                    copy_pT_b(c, 2)
                if a is not None:
                    copy_q(a, 1)
                if c is not None:
                    copy_pT_b(c, 3)
                if a is not None:
                    exps_a(a, 0)
                if b is not None:
                    mask_k(b)
                if a is not None:
                    copy_v(a)
                    exps_a(a, 1)
                if b is not None:
                    exps_b(b, 0)
                if a is not None:
                    turn_next(a)
                    exps_a(a, 2)
                if b is not None:
                    exps_b(b, 1)
                if a is not None:
                    exps_a(a, 3)
                if c is not None:
                    exp_logits(c)
                if b is not None:
                    copy_pT_b(b, 0)
                    exps_b(b, 2)
                    copy_pT_b(b, 1)
                    exps_b(b, 3)

            def drain(b, c):
                if c is not None:
                    copy_pT_b(c, 2)
                    copy_pT_b(c, 3)
                if b is not None:
                    mask_k(b)
                if c is not None:
                    exp_logits(c)
                if b is not None:
                    exps_b(b, 0)
                    exps_b(b, 1)
                    exps_b(b, 2)
                    copy_pT_b(b, 0)
                    exps_b(b, 3)
                    copy_pT_b(b, 1)

            def fill_pipe(a):
                copy_q(a, 0)
                copy_q(a, 1)
                copy_k(a, 0)
                copy_k(a, 1)
                exps_a(a, 0)
                exps_a(a, 1)
                turn_next(a)
                copy_v(a)
                exps_a(a, 2)
                exps_a(a, 3)
            batches(act, body, drain, fill_pipe)
            for e in range(NE):
                for m in range(MT):
                    h_made.wait(act, e, m // 2 + 1)
                    if m == 0 and e >= 2:
                        e_made.wait(act, e - 2)
                    hb = bk[1 + 2 * (e % 2) + m // 2]
                    nc.scalar.activation(hid[:, e % 2, m, :], hb[:, (m % 2) * 256:(m % 2) * 256 + 256], ACT.Gelu,
                                         bias=cols[:, 4 + e * MT + m:5 + e * MT + m]).then_inc(h_act.sem, 1)
            for half in range(2):
                d_eo[half].wait(act, NE // 2 - 1)
            for n in range(1, NB, 2):
                act.dma_start(got[:, n, :, :], results[n * TOPK * P:(n + 1) * TOPK * P, :].rearrange("(k p) d -> p k d", p=P)
                              ).then_inc(d_got[n].sem, 16)

        @block.vector
        def _(dve):
            n_prep = [0]

            def link(ins):
                n_prep[0] += 1
                ins.then_inc(prep, 1)
                dve.wait_ge(prep, n_prep[0])

            def variances(first, last):
                for n in range(first, last):
                    ins = nc.vector.bn_stats(stats_x[:, n, :], x_all[:, n, :])
                link(ins)
                for n in range(first, last):
                    ins = nc.vector.bn_aggr(mv_x[:, n, :], stats_x[:, n, :])
                link(ins)
                nc.vector.tensor_scalar(ve_x[:, first:last], mv_x[:, first:last, 1], EPS, None, ALU.add).then_inc(vars_ready, 1)

            def apply_xn(a):
                nc.vector.tensor_scalar(xn[:], x_all[:, a, :], mv_x[:, a, 0:1], rstd_x[:, bass.ds(a, 1)],
                                        ALU.subtract, ALU.mult).then_inc(xn_ready.sem, 1)

            dve.wait_ge(d_x0, 16)
            variances(0, 1)
            dve.wait_ge(d_cst, 16)
            nc.vector.tensor_copy(ident_bf[:], ident)
            nc.vector.tensor_copy(tri_bf[:], cst[:, C_TRI:C_TRI + P])
            link(nc.vector.tensor_copy(causal_bf[:], cst[:, C_CAUSAL:C_CAUSAL + P]))
            dve.wait_ge(rstd_ready, 1)
            apply_xn(0)
            dve.wait_ge(blank_zero, 1)
            nc.vector.tensor_copy(blank[:, :, P], cst[:, C_FREE:C_FREE + QR]).then_inc(zeroed, 1)
            dve.wait_ge(d_x, 16)
            variances(1, NB)
            dve.wait_ge(d_mask, 16)
            link(nc.vector.tensor_scalar(mask_neg[:], mask_i32[:], NEG, None, ALU.mult))
            nc.vector.tensor_tensor(mask_all[:].rearrange("p (b t) -> p b t", b=NB),
                                    mask_neg[:].rearrange("p (b t) -> p b t", b=NB),
                                    causal_bf[:].unsqueeze(1).broadcast_to([P, NB, P]), ALU.min).then_inc(consts_ready, 1)
            dve.wait_ge(prep_pool, 5)

            def weight_columns():
                dve.wait_ge(d_wqkv, 16)
                src = wqkv_sb[:].rearrange("p (h s d) -> p s h d", h=SH, s=3)
                for s in range(2):
                    dst = w4_sb[:, s, :].rearrange("p (h d) -> p h d", h=SH)
                    rot = w4_sb[:, 2 + s, :].rearrange("p (h d) -> p h d", h=SH)
                    nc.vector.tensor_copy(dst, src[:, s])
                    nc.vector.tensor_scalar(rot[:, :, 0:SD // 2], src[:, s, :, SD // 2:SD], -1.0, None, ALU.mult)
                    nc.vector.tensor_copy(rot[:, :, SD // 2:SD], src[:, s, :, 0:SD // 2])
                nc.vector.tensor_copy(wvs_sb[:].rearrange("p (h d) -> p h d", h=SH), src[:, 2]).then_inc(w4_ready, 1)

            def spare_dve():
                nc.vector.memset(tiny[:, 0:1], 0.0)

            a_links, b_links, c_links = Chain(dve, a_chain), Chain(dve, b_chain), Chain(dve, c_chain)

            def row_max(batch, k, bank_, nmax, scores_s, max_s):
                scores_s.wait(dve, batch, k + 1)
                nc.vector.tensor_reduce(nmax[:, HC * k:HC * k + HC], bank_[:].rearrange("p (h t) -> p h t", h=HC),
                                        AX.X, ALU.max, negate=True).then_inc(max_s.sem, 1)

            def recip(batch, k, sums, rec, exp_s, rec_s):
                exp_s.wait(dve, batch, k + 1)
                nc.vector.reciprocal(rec[:, HC * k:HC * k + HC], sums[:, HC * k:HC * k + HC]).then_inc(rec_s.sem, 1)

            def recip_a(a, k):
                recip(a, k, sum_a, rec_a, a_exp, a_rec)

            def recip_b(b, k):
                recip(b, k, sum_b, rec_b, b_exp, b_rec)

            def max_a(a, k):
                row_max(a, k, sa_banks(a)[k % 2], nmax_a, a_scores, a_max)

            def max_b(b, k):
                row_max(b, k, s_banks(b)[k % 2], nmax_b, b_scores, b_max)

            def copy_pT_a(a, k):
                a_turned.wait(dve, a, k + 1)
                nc.vector.tensor_copy(pT_a[:, k % 2].rearrange("p h t -> p (h t)"), ta_banks(a)[k % 2][:]).then_inc(a_pT.sem, 1)

            def copy_oT_a(a, half):
                a_pv.wait(dve, a, 2 * half + 2)
                nc.vector.tensor_copy(oT_a[:].rearrange("p m t -> p (m t)"), o_a[:]).then_inc(a_oT.sem, 1)

            def copy_k(a, f):
                k_made.wait(dve, a, f + 1)
                nc.vector.tensor_copy(kz[0:XD, 4 * f:4 * f + 4, 0, :],
                                      k_banks[f][0:XD, :].rearrange("p (m t) -> p m t", m=4)).then_inc(k_ready0.sem, 1)

            def x1_var(b):
                a_links.start(b)
                if isinstance(b, int) and b == 0:
                    dve.wait_ge(xb_ready, 1)
                a_y.wait(dve, b)
                nc.vector.scalar_tensor_tensor(out=x1_all[:, b, :], in0=y_bank[:, 0:P], scalar=tanh2[:, 0:1],
                                               in1=x1_all[:, b, :], op0=ALU.mult, op1=ALU.add).then_inc(a_x1.sem, 1)
                a_x1.wait(dve, b, carrier=spare_dve)
                a_links.link(nc.vector.bn_stats(st_a[:, 0, :], x1_all[:, b, :]), spare_dve)
                a_links.link(nc.vector.bn_aggr(mv_a[:, 0, :], st_a[:, 0, :]))
                nc.vector.tensor_scalar(ve_a[:, 0:1], mv_a[:, 0, 1:2], EPS, None, ALU.add).then_inc(a_var.sem, 1)

            def z_var(b):
                a_rstd.wait(dve, b, 1)
                a_links.link(nc.vector.tensor_scalar(z_all[:, b, :], x1_all[:, b, :], mv_a[:, 0, 0:1], rs_a[:, 0:1],
                                                     ALU.subtract, ALU.mult), spare_dve)
                a_links.link(nc.vector.bn_stats(st_a[:, 1, :], z_all[:, b, :]), spare_dve)
                a_links.link(nc.vector.bn_aggr(mv_a[:, 1, :], st_a[:, 1, :]))
                nc.vector.tensor_scalar(ve_a[:, 1:2], mv_a[:, 1, 1:2], EPS, None, ALU.add).then_inc(a_var.sem, 1)
                a_links.end()

            def norm_h(b):
                a_rstd.wait(dve, b, 2)
                nc.vector.tensor_scalar(h_sb[:], z_all[:, b, :], mv_a[:, 1, 0:1], rs_a[:, 1:2],
                                        ALU.subtract, ALU.mult).then_inc(h_ready.sem, 1)

            def copy_hT(b):
                if isinstance(b, int) and b == 0:
                    dve.wait_ge(rows_turned, 1)
                    nc.vector.tensor_copy(cols[:], c_bank[:, 3 * P:3 * P + NV]).then_inc(cols_ready, 1)
                    dve.wait_ge(cols_ready, 1)
                h_turned.wait(dve, b)
                nc.vector.tensor_scalar(hT[:], c_bank[:, 0:P], cols[:, 0:1], cols[:, 1:2],
                                        ALU.mult, ALU.add).then_inc(hT_ready.sem, 1)

            def copy_oT_b(c):
                b_pv.wait(dve, c)
                nc.vector.tensor_copy(oT_b[:], o_b[:, 0:P]).then_inc(b_oT.sem, 1)

            def x2_var(c):
                b_links.start(c)
                b_proj.wait(dve, c)
                nc.vector.tensor_tensor(z_all[:, c, :], o_b[:, 2 * P:3 * P], z_all[:, c, :], ALU.add).then_inc(b_x2.sem, 1)
                b_x2.wait(dve, c, carrier=spare_dve)
                b_links.link(nc.vector.bn_stats(st_b[:], z_all[:, c, :]), spare_dve)
                b_links.link(nc.vector.bn_aggr(mv_b[:], st_b[:]))
                b_links.end()
                nc.vector.tensor_scalar(ve_b[:], mv_b[:, 1:2], EPS, None, ALU.add).then_inc(b_var.sem, 1)

            def norm_h2(c):
                b_rstd.wait(dve, c)
                nc.vector.tensor_scalar(h2n[:], z_all[:, c, :], mv_b[:, 0:1], rs_b[:, 0:1],
                                        ALU.subtract, ALU.mult).then_inc(h2n_ready.sem, 1)

            def copy_v(a):
                v_made.wait(dve, a, 2)
                nc.vector.tensor_copy(v_sb[:, 512:1024], v_banks[1][:]).then_inc(v_ready1.sem, 1)

            def next_xn(a):
                if isinstance(a, int) and a == 0:
                    weight_columns()
                    dve.wait_ge(rstd_ready, 2)
                if has_next(a):
                    apply_xn(a + 1)

            def rope_mul(b):
                qk_made.wait(dve, b)
                nc.vector.tensor_tensor(rope1[:], y_bank[:, 0:2 * P], cos_qk, ALU.mult)
                nc.vector.tensor_tensor(rope2[:], y_bank[:, 2 * P:4 * P], sin_qk, ALU.mult).then_inc(qk_read.sem, 1)

            def rope_add(b):
                qk_read.wait(dve, b)
                nc.vector.tensor_tensor(kr[:], rope1[:, P:2 * P], rope2[:, P:2 * P], ALU.add).then_inc(rope_ready.sem, 1)
                for g in range(4):
                    r = slice(32 * g, 32 * g + 32)
                    last = nc.vector.tensor_tensor(qz[r, g, :], rope1[r, 0:P], rope2[r, 0:P], ALU.add)
                last.then_inc(qz_ready.sem, 1)

            def copy_vs(b):
                vs_made.wait(dve, b)
                nc.vector.tensor_copy(v_diag, c_bank[:, P:2 * P].rearrange("p (g j d) -> p g j d", g=4, j=HC)
                                      ).then_inc(vs_ready.sem, 1)

            def body(a, b, c):
                if a is not None:
                    next_xn(a)
                if b is not None:
                    x1_var(b)
                    z_var(b)
                if a is not None:
                    copy_k(a, 0)
                    copy_k(a, 1)
                if b is not None:
                    norm_h(b)
                    copy_hT(b)
                if a is not None:
                    max_a(a, 0)
                if b is not None:
                    rope_mul(b)
                if c is not None:
                    copy_oT_b(c)
                if b is not None:
                    rope_add(b)
                if a is not None:
                    max_a(a, 1)
                    recip_a(a, 0)
                if c is not None:
                    x2_var(c)
                if b is not None:
                    max_b(b, 0)
                if c is not None:
                    norm_h2(c)
                if b is not None:
                    copy_vs(b)
                if a is not None:
                    recip_a(a, 1)
                    max_a(a, 2)
                    copy_pT_a(a, 0)
                if c is not None:
                    copy_h2T(c)
                if b is not None:
                    max_b(b, 1)
                if a is not None:
                    recip_a(a, 2)
                    copy_pT_a(a, 1)
                if b is not None:
                    recip_b(b, 0)
                if a is not None:
                    copy_v(a)
                    max_a(a, 3)
                if b is not None:
                    recip_b(b, 1)
                if a is not None:
                    copy_oT_a(a, 0)
                    copy_pT_a(a, 2)
                if c is not None:
                    max_logits(c)
                if a is not None:
                    recip_a(a, 3)
                if b is not None:
                    max_b(b, 2)
                if c is not None:
                    choose(c)
                if a is not None:
                    copy_pT_a(a, 3)
                if b is not None:
                    recip_b(b, 2)
                if c is not None:
                    place(c)
                if b is not None:
                    max_b(b, 3)
                if a is not None:
                    copy_oT_a(a, 1)
                if b is not None:
                    recip_b(b, 3)

            def drain(b, c):
                if b is not None:
                    x1_var(b)
                    z_var(b)
                if c is not None:
                    copy_oT_b(c)
                if b is not None:
                    norm_h(b)
                    copy_hT(b)
                if c is not None:
                    x2_var(c)
                if b is not None:
                    rope_mul(b)
                if c is not None:
                    norm_h2(c)
                if b is not None:
                    rope_add(b)
                    copy_vs(b)
                if c is not None:
                    copy_h2T(c)
                if b is not None:
                    max_b(b, 0)
                if c is not None:
                    max_logits(c)
                    choose(c)
                if b is not None:
                    max_b(b, 1)
                    recip_b(b, 0)
                    max_b(b, 2)
                    recip_b(b, 1)
                if c is not None:
                    place(c)
                if b is not None:
                    recip_b(b, 2)
                    max_b(b, 3)
                    recip_b(b, 3)

            def fill_pipe(a):
                copy_k(a, 0)
                copy_k(a, 1)
                next_xn(a)
                max_a(a, 0)
                max_a(a, 1)
                recip_a(a, 0)
                max_a(a, 2)
                recip_a(a, 1)
                copy_pT_a(a, 0)
                copy_v(a)
                max_a(a, 3)
                recip_a(a, 2)
                copy_pT_a(a, 1)
                recip_a(a, 3)
                copy_pT_a(a, 2)
                copy_oT_a(a, 0)
                copy_pT_a(a, 3)
                copy_oT_a(a, 1)

            v_diag = v_pad[:].rearrange("p (g j) c -> p g (j c)", g=4)
            v_diag = bass.AP(tensor=v_diag.tensor, offset=v_diag.offset,
                             ap=[list(v_diag.ap[0]), [HC * HC * SD, 4], [HC * SD + SD, HC], [1, SD]])

            def copy_h2T(c):
                h2_turned.wait(dve, c)
                nc.vector.tensor_scalar(h2T[:], c_bank[:, 0:P], cols[:, 2:3], cols[:, 3:4],
                                        ALU.mult, ALU.add).then_inc(h2T_ready.sem, 1)

            def max_logits(c):
                logits_made.wait(dve, c)
                nc.vector.tensor_reduce(r_nmax[:], c_bank[:, P:P + NE], AX.X, ALU.max, negate=True).then_inc(lmax_ready.sem, 1)

            def choose(c):
                c_links.start(c)
                lexp_ready.wait(dve, c)
                c_links.link(nc.vector.reciprocal(r_rec[:], r_sum[:]))
                c_links.link(nc.vector.tensor_scalar(r_gate[:], r_exp[:], r_rec[:, 0:1], None, ALU.mult), spare_dve)
                c_links.link(nc.vector.max(r_top[:], r_gate[:]), spare_dve)
                c_links.link(nc.vector.max_index(r_idx[:], r_top[:], r_gate[:]))
                c_links.link(nc.vector.tensor_copy(r_idxf[:], r_idx[:, 0:TOPK]))
                c_links.link(nc.vector.tensor_tensor(r_mk[:], iota2, r_idxf[:].unsqueeze(2).broadcast_to([P, TOPK, NE]),
                                                     ALU.is_equal))
                nc.vector.tensor_tensor(r_mask[:], r_mk[:, 0, :], r_mk[:, 1, :], ALU.add).then_inc(choice_ready.sem, 1)

            def place(c):
                pos_made.wait(dve, c)
                nc.vector.tensor_tensor(r_pm[:], r_mk[:], c_bank[:, 256:256 + NE].unsqueeze(1).broadcast_to([P, TOPK, NE]),
                                        ALU.mult).then_inc(pos_read.sem, 1)
                pos_read.wait(dve, c)
                nc.vector.tensor_tensor(r_acc[:], r_acc[:], r_mask[:], ALU.add)
                c_links.link(nc.vector.tensor_reduce(r_pos[:], r_pm[:], AX.X, ALU.add))
                nc.vector.scalar_tensor_tensor(out=gate_all[:, c, :], in0=r_pos[:], scalar=float(CAP),
                                               in1=r_top[:, 0:TOPK], op0=ALU.is_le, op1=ALU.mult)
                nc.vector.tensor_scalar(r_keep[:], r_pos[:], float(CAP), None, ALU.is_le)
                nc.vector.scalar_tensor_tensor(out=r_drop[:], in0=r_pos[:], scalar=float(CAP),
                                               in1=cst_trash(c), op0=ALU.is_gt, op1=ALU.mult)
                c_links.link(nc.vector.tensor_scalar(r_pmin[:], r_pos[:], float(CAP), -1.0, ALU.min, ALU.add))
                c_links.link(nc.vector.scalar_tensor_tensor(out=r_row[:], in0=r_idxf[:], scalar=float(CAP), in1=r_pmin[:],
                                                            op0=ALU.mult, op1=ALU.add))
                c_links.link(nc.vector.tensor_tensor(r_kept[:], r_row[:], r_keep[:], ALU.mult))
                c_links.link(nc.vector.tensor_tensor(r_row[:], r_kept[:], r_drop[:], ALU.add))
                if later(c):
                    d_scatter.wait(dve, c - 1)
                nc.vector.tensor_scalar(h2s[:, :, P], cst_trash(c), -float(NE * CAP), None, ALU.add)
                nc.vector.tensor_copy(r_slot[:], r_row[:]).then_inc(slots_ready.sem, 1)
                c_links.end()

            trash = cst[:, C_TRASH:C_TRASH + 2 * NB].rearrange("p (b k) -> p b k", k=TOPK)

            def cst_trash(c):
                return trash[:, c, :]

            batches(dve, body, drain, fill_pipe)

            dve.wait_ge(d_b2, 16)

            def turned(e):
                x_turned.wait(dve, e)
                nc.vector.tensor_copy(dest[:, e, :], xin[:, e % RING, :, P])
                nc.vector.tensor_scalar(xT[:, e % 2, :], bk[0][:, 0:2 * P], cols[:, 2:3], cols[:, 3:4],
                                        ALU.mult, ALU.add).then_inc(xT_ready.sem, 1)
            turned(0)
            turned(1)
            nc.vector.tensor_scalar(gate_t[:], gate_all[:], tanh2[:, 1:2], None, ALU.mult)
            nc.vector.scalar_tensor_tensor(out=x1_all[:], in0=z_all[:], scalar=tanh2[:, 1:2], in1=x1_all[:],
                                           op0=ALU.mult, op1=ALU.add).then_inc(base_ready, 1)
            for e in range(NE):
                if e + 2 < NE:
                    turned(e + 2)
                e_made.wait(dve, e)
                if e >= 2:
                    d_eo[e % 2].wait(dve, e // 2 - 1)
                nc.vector.tensor_tensor(eo[:, e % 2, :, :], bk[5 + e % 2][:, 0:2 * P].rearrange("p (t d) -> p t d", t=2),
                                        b2_bc[:, e, :].unsqueeze(1).broadcast_to([P, 2, P]), ALU.add).then_inc(eo_ready.sem, 1)
            dve.wait_ge(base_ready, 1)

            def second(n):
                half_mixed.wait(dve, n)
                nc.vector.scalar_tensor_tensor(out=res[:, n, :], in0=got[:, n, 1, :], scalar=gate_t[:, n, 1:2],
                                               in1=acc[:, n, :], op0=ALU.mult, op1=ALU.add).then_inc(mixed.sem, 1)

            for n in range(NB):
                d_got[n].wait(dve, 0)
                nc.vector.scalar_tensor_tensor(out=acc[:, n, :], in0=got[:, n, 0, :], scalar=gate_t[:, n, 0:1],
                                               in1=x1_all[:, n, :], op0=ALU.mult, op1=ALU.add).then_inc(half_mixed.sem, 1)
                if n >= 1:
                    second(n - 1)
            second(NB - 1)

        @block.tensor
        def _(pe):
            def turn_xc(a):
                xn_ready.wait(pe, a)
                d_ctx.wait(pe, a)
                nc.tensor.transpose(o_b[:, 0:P], xn[:], ident)
                nc.tensor.transpose(o_b[:, P:2 * P], c_sb[:], ident).then_inc(xc_turned.sem, 1)

            pe.wait_ge(d_cst, 16)
            turn_xc(0)

            def fill(a, w, half, banks, made, f):
                for m in range(4):
                    last = nc.tensor.matmul(banks[f][:, m * P:(m + 1) * P], w[:, (4 * f + m) * P:(4 * f + m + 1) * P],
                                            xcT[:, half * P:(half + 1) * P], start=True, stop=True)
                last.then_inc(made.sem, 1)

            def fill_q(a, f):
                if f == 0:
                    xcT_ready.wait(pe, a)
                    if isinstance(a, int) and a == 0:
                        pe.wait_ge(d_wq, 16)
                if later(a):
                    (a_exp, a_oT)[f].wait(pe, a - 1)
                fill(a, wq_sb, 0, q_banks, q_made, f)

            def fill_k(a, f):
                xcT_ready.wait(pe, a)
                if isinstance(a, int) and a == 0:
                    pe.wait_ge(d_wk, 16)
                if later(a):
                    (a_pT, a_x1)[f].wait(pe, a - 1)
                fill(a, wk_sb, 1, k_banks, k_made, f)

            def fill_v(a, f):
                if f == 0:
                    q_ready.wait(pe, a)
                if isinstance(a, int) and a == 0:
                    pe.wait_ge(d_wv, 16)
                if f == 1 and (not isinstance(a, int) or a >= 2):
                    b_pT.wait(pe, a - 2)
                if f == 1 and isinstance(a, int) and a == 1:
                    a_pT.wait(pe, 0)
                nc.tensor.matmul(v_banks[f][:], xcT[:, P:2 * P], wv_sb[:, f * 512:(f + 1) * 512],
                                 start=True, stop=True).then_inc(v_made.sem, 1)

            def turn_h(b):
                if isinstance(b, int) and b == 0:
                    pe.wait_ge(d_rows, 80)
                    nc.tensor.transpose(c_bank[:, 3 * P:3 * P + NV], rows[:], ident[0:NV, 0:NV]).then_inc(rows_turned, 1)
                    pe.wait_ge(cols_ready, 1)
                h_ready.wait(pe, b)
                if later(b):
                    if not isinstance(b, int) or b >= 2:
                        pos_read.wait(pe, b - 2)
                nc.tensor.transpose(c_bank[:, 0:P], h_sb[:], ident).then_inc(h_turned.sem, 1)

            def project_b(b):
                hT_ready.wait(pe, b)
                if isinstance(b, int) and b == 0:
                    pe.wait_ge(w4_ready, 1)
                if has_next(b):
                    k_ready0.wait(pe, b + 1)
                    k_ready1.wait(pe, b + 1)
                else:
                    a_x1.wait(pe, b)
                for n in range(4):
                    last = nc.tensor.matmul(y_bank[:, n * P:(n + 1) * P], w4_sb[:, n, :], hT[:], start=True, stop=True)
                last.then_inc(qk_made.sem, 1)
                nc.tensor.matmul(c_bank[:, P:2 * P], hT[:], wvs_sb[:], start=True, stop=True).then_inc(vs_made.sem, 1)

            def scores_a(a, k):
                if k == 0:
                    if isinstance(a, int) and a == 0:
                        pe.wait_ge(consts_ready, 1)
                    q_ready.wait(pe, a)
                    k_ready0.wait(pe, a)
                    k_ready1.wait(pe, a)
                elif later(a):
                    a_exp.wait(pe, a, k)
                elif k >= 2:
                    a_exp.wait(pe, a, k - 1)
                bank_ = sa_banks(a)[k % 2]
                nc.tensor.matmul(bank_[:], ident_bf[:], mask_all[:, bass.ts(a, P)].unsqueeze(1).broadcast_to([P, HC, P]),
                                 start=True, stop=False, skip_group_check=True)
                for n in range(2):
                    m = 2 * k + n
                    last = nc.tensor.matmul(bank_[:, n * 2 * P:(n + 1) * 2 * P], qT[:, m, :],
                                            kz[:, m, :, :].rearrange("p s t -> p (s t)"),
                                            start=False, stop=True, skip_group_check=True)
                last.then_inc(a_scores.sem, 1)

            def scores_b(b, k):
                bank_ = s_banks(b)[k % 2]
                if k == 0:
                    if not later(b):
                        a_exp.wait(pe, b)
                    qz_ready.wait(pe, b)
                    qkm_ready.wait(pe, b)
                elif s_banks(b)[0] is s_banks(b)[1]:
                    b_exp.wait(pe, b, k)
                elif k == 1:
                    a_exp.wait(pe, b)
                else:
                    b_exp.wait(pe, b, k - 1)
                nc.tensor.matmul(bank_[:], ident_bf[:], causal_bf[:].unsqueeze(1).broadcast_to([P, HC, P]),
                                 start=True, stop=False, skip_group_check=True)
                nc.tensor.matmul(bank_[:], qz[:, k, :], km[:].rearrange("p h t -> p (h t)"),
                                 start=False, stop=True, skip_group_check=True).then_inc(b_scores.sem, 1)

            def turn_p(batch, k, banks, p_buf, norm_s, pT_s, turned_s):
                norm_s.wait(pe, batch, k + 1)
                bank_ = banks[k % 2]
                if banks[0] is banks[1] and k >= 1:
                    pT_s.wait(pe, batch, k)
                elif k >= 2:
                    pT_s.wait(pe, batch, k - 1)
                for j in range(HC):
                    last = nc.tensor.transpose(bank_[:, j * P:(j + 1) * P], p_buf[:, k % 2, j, :], ident)
                last.then_inc(turned_s.sem, 1)

            def turn_a(a, k):
                if k == 1 and not later(a):
                    v_ready1.wait(pe, a)
                turn_p(a, k, ta_banks(a), p_a, a_norm, a_pT, a_turned)

            def turn_b(b, k):
                if not has_next(b) and k == 1:
                    a_pT.wait(pe, b)
                if k == 0 and has_next(b):
                    v_ready1.wait(pe, b + 1)
                turn_p(b, k, t_banks(b), p_b, b_norm, b_pT, b_turned)

            def pv_a(a, k):
                a_pT.wait(pe, a, k + 1)
                if k == 0:
                    v_ready0.wait(pe, a)
                if k == 2:
                    v_ready1.wait(pe, a)
                    a_oT.wait(pe, a, 1)
                for j in range(HC):
                    h = HC * k + j
                    r, m = XD * (h % 2), (h // 2) % 4
                    last = nc.tensor.matmul(o_a[r:r + XD, m * P:(m + 1) * P], v_sb[:, h * XD:(h + 1) * XD], pT_a[:, k % 2, j, :],
                                            start=True, stop=True)
                last.then_inc(a_pv.sem, 1)

            def pv_b(b, g):
                b_pT.wait(pe, b, g + 1)
                if g == 0:
                    vs_ready.wait(pe, b)
                    if not isinstance(b, int) or b + 2 < NB:
                        xcT_ready.wait(pe, b + 2)
                for j in range(HC):
                    last = nc.tensor.matmul(o_b[32 * g:32 * g + 32, 0:P], v_pad[:, HC * g + j, :], pT_b[:, g % 2, j, :],
                                            start=(j == 0), stop=(j == HC - 1))
                if g == CHUNKS - 1:
                    last.then_inc(b_pv.sem, 1)

            def output_a(a, half):
                a_oT.wait(pe, a, half + 1)
                if half == 0 and later(a):
                    qk_read.wait(pe, a - 1)
                if isinstance(a, int) and a == 0:
                    pe.wait_ge(d_wo, 16)
                for m in range(4):
                    last = nc.tensor.matmul(y_bank[:, 0:P], oT_a[:, m, :], wo_sb[:, 4 * half + m, :],
                                            start=(half == 0 and m == 0), stop=(half == 1 and m == 3))
                if half == 1:
                    last.then_inc(a_y.sem, 1)

            def output_b(c):
                if isinstance(c, int) and c == 0:
                    pe.wait_ge(d_proj, 32)
                b_oT.wait(pe, c)
                nc.tensor.matmul(o_b[:, 2 * P:3 * P], oT_b[:], wproj_sb[:], start=True, stop=True).then_inc(b_proj.sem, 1)

            def turn_h2(c):
                if has_next(c):
                    vs_ready.wait(pe, c + 1)
                h2n_ready.wait(pe, c)
                nc.tensor.transpose(c_bank[:, 0:P], h2n[:], ident).then_inc(h2_turned.sem, 1)

            def logits(c):
                h2T_ready.wait(pe, c)
                nc.tensor.matmul(c_bank[:, P:P + NE], h2T[:], wgate_sb[:], start=True, stop=True).then_inc(logits_made.sem, 1)

            def turn_next(a):
                if has_next(a):
                    if not isinstance(a, int) or a >= 2:
                        b_x2.wait(pe, a - 2)
                    turn_xc(a + 1)

            def positions(c):
                choice_ready.wait(pe, c)
                nc.tensor.matmul(c_bank[:, 256:256 + NE], tri_bf[:], r_mask[:], start=True, stop=False)
                nc.tensor.matmul(c_bank[:, 256:256 + NE], ones_bf[:], r_acc[:], start=False, stop=True).then_inc(pos_made.sem, 1)

            def body(a, b, c):
                if a is not None:
                    fill_q(a, 0)
                    fill_k(a, 0)
                    fill_k(a, 1)
                if c is not None:
                    turn_b(c, 2)
                if a is not None:
                    fill_q(a, 1)
                if c is not None:
                    turn_b(c, 3)
                if b is not None:
                    turn_h(b)
                if a is not None:
                    scores_a(a, 0)
                if b is not None:
                    project_b(b)
                if c is not None:
                    pv_b(c, 2)
                    pv_b(c, 3)
                if a is not None:
                    fill_v(a, 0)
                    scores_a(a, 1)
                if c is not None:
                    output_b(c)
                if b is not None:
                    scores_b(b, 0)
                if a is not None:
                    fill_v(a, 1)
                    turn_next(a)
                    scores_a(a, 2)
                if c is not None:
                    turn_h2(c)
                if a is not None:
                    turn_a(a, 0)
                if b is not None:
                    scores_b(b, 1)
                if a is not None:
                    turn_a(a, 1)
                    pv_a(a, 0)
                if c is not None:
                    logits(c)
                if a is not None:
                    scores_a(a, 3)
                    pv_a(a, 1)
                    turn_a(a, 2)
                if b is not None:
                    scores_b(b, 2)
                    turn_b(b, 0)
                if a is not None:
                    pv_a(a, 2)
                    output_a(a, 0)
                    turn_a(a, 3)
                if b is not None:
                    turn_b(b, 1)
                if c is not None:
                    positions(c)
                if b is not None:
                    scores_b(b, 3)
                if a is not None:
                    pv_a(a, 3)
                if b is not None:
                    pv_b(b, 0)
                    pv_b(b, 1)
                if a is not None:
                    output_a(a, 1)

            def drain(b, c):
                if c is not None:
                    turn_b(c, 2)
                    turn_b(c, 3)
                    pv_b(c, 2)
                    pv_b(c, 3)
                if b is not None:
                    turn_h(b)
                if c is not None:
                    output_b(c)
                if b is not None:
                    project_b(b)
                if c is not None:
                    turn_h2(c)
                if b is not None:
                    scores_b(b, 0)
                if c is not None:
                    logits(c)
                if b is not None:
                    scores_b(b, 1)
                if c is not None:
                    positions(c)
                if b is not None:
                    scores_b(b, 2)
                    turn_b(b, 0)
                    scores_b(b, 3)
                    turn_b(b, 1)
                    pv_b(b, 0)
                    pv_b(b, 1)

            def fill_pipe(a):
                fill_q(a, 0)
                fill_q(a, 1)
                fill_k(a, 0)
                fill_k(a, 1)
                fill_v(a, 0)
                scores_a(a, 0)
                scores_a(a, 1)
                fill_v(a, 1)
                turn_next(a)
                scores_a(a, 2)
                turn_a(a, 0)
                scores_a(a, 3)
                turn_a(a, 1)
                pv_a(a, 0)
                turn_a(a, 2)
                pv_a(a, 1)
                turn_a(a, 3)
                output_a(a, 0)
                pv_a(a, 2)
                pv_a(a, 3)
                output_a(a, 1)
            batches(pe, body, drain, fill_pipe)

            def turn_x(e):
                d_xin[e % RING].wait(pe, e // RING)
                if e >= 1:
                    xT_ready.wait(pe, e - 1)
                for t in range(2):
                    last = nc.tensor.transpose(bk[0][:, t * P:(t + 1) * P], xin[:, e % RING, t, 0:P], ident)
                last.then_inc(x_turned.sem, 1)

            def hidden(e):
                xT_ready.wait(pe, e)
                d_w[e % RING].wait(pe, e // RING)
                if e >= 2:
                    h_act.wait(pe, e - 2)
                for m in range(MT):
                    last = nc.tensor.matmul(bk[1 + 2 * (e % 2) + m // 2][:, (m % 2) * 256:(m % 2) * 256 + 256],
                                            w1_sb[:, e % RING, m * P:(m + 1) * P], xT[:, e % 2, :], start=True, stop=True)
                    if m % 2:
                        last.then_inc(h_made.sem, 1)

            def expert_out(e):
                h_act.wait(pe, e)
                if e >= 2:
                    eo_ready.wait(pe, e - 2)
                for t in range(2):
                    for m in range(MT):
                        last = nc.tensor.matmul(bk[5 + e % 2][:, t * P:(t + 1) * P], hid[:, e % 2, m, t * P:(t + 1) * P],
                                                w2_sb[:, e % RING, m, :], start=(m == 0), stop=(m == MT - 1))
                last.then_inc(e_made.sem, 1)

            turn_x(0)
            for e in range(NE):
                hidden(e)
                if e + 1 < NE:
                    turn_x(e + 1)
                if e >= 1:
                    expert_out(e - 1)
            expert_out(NE - 1)


def constants():
    import numpy as np
    c = np.zeros((P, NCONST), np.float32)
    p, t = np.arange(P)[:, None], np.arange(P)[None, :]
    c[:, C_ID:C_ID + P] = p == t
    c[:, C_CAUSAL:C_CAUSAL + P] = np.where(t > p, np.float32(NEG), np.float32(0))
    c[:, C_TRI:C_TRI + P] = p <= t
    freq = (np.float32(1) / np.float32(10000) ** (np.arange(0, SD, 2, dtype=np.float32) / np.float32(SD))).astype(np.float32)
    angle = freq[np.arange(P) % (SD // 2)][:, None] * np.arange(P, dtype=np.float32)[None, :]
    for at, f in ((C_COS, np.cos), (C_SIN, np.sin)):
        c[:, at:at + P] = f(angle) * np.float32(SD ** -0.5)
        c[:, at + P:at + 2 * P] = f(angle)
    c[:, C_HMASK:C_HMASK + HC] = (p // SD) % HC == np.arange(HC)[None, :]
    c[:, C_IOTA:C_IOTA + 2 * NE] = np.tile(np.arange(NE), 2)[None, :]
    c[:, C_TRASH:C_TRASH + 2 * NB] = NE * CAP + np.arange(2 * NB)[None, :] * P + p
    c[:, C_POW:C_POW + NB] = -0.5
    c[:, C_FREE:C_FREE + QR] = NB * TOPK * P + QR * p + np.arange(QR)[None, :]
    return c


_INS = ['x', 'ctx_1024', 'mask_BxS2_bf0', 'g_xattn', 'g_ffn', 'L0_xattn_Wq', 'L0_xattn_Wk', 'L0_xattn_Wv', 'L0_xattn_Wo',
        'L0_xattn_bo', 'L0_ffn_ln1_g', 'L0_ffn_ln1_b', 'L0_ffn_Wqkv', 'L0_ffn_Wproj', 'L0_ffn_ln2_g', 'L0_ffn_ln2_b',
        'L0_ffn_Wgate', 'L0_ffn_W1', 'L0_ffn_b1', 'L0_ffn_W2', 'L0_ffn_b2']


def kernel(**inputs):
    import numpy as _np
    import concourse.bacc as _bacc
    from concourse import mybir as _mybir
    from concourse.bass_utils import run_bass_kernel_spmd as _run

    nc = _bacc.Bacc("TRN2", target_bir_lowering=False, num_devices=1)
    arrays, args = {}, []
    for name in _INS:
        a = _np.ascontiguousarray(inputs[name])
        if a.dtype.kind == "b":
            a = a.astype(_np.int32)
        arrays[f"in_{name}"] = a
    arrays["in_const"] = constants()
    for name, a in arrays.items():
        args.append(nc.dram_tensor(name, a.shape, _mybir.dt.from_np(a.dtype), kind="ExternalInput").ap())
    args.append(nc.dram_tensor("out_0", (NB, P, P), _mybir.dt.float32, kind="ExternalOutput").ap())
    build(nc, *args)
    r = _run(nc, [arrays], core_ids=[0])
    return r.results[0]["out_0"]
```
